# Optimizing a Trainium2 kernel written in Bass

```python
import numpy as np
import jax
import jax.numpy as jnp

def _softmax(x, axis=-1):
    return jax.nn.softmax(x, axis=axis)

def _gelu(x):
    return jax.nn.gelu(x, approximate=True)

def _silu(x):
    return jax.nn.silu(x)

def _sigmoid(x):
    return jax.nn.sigmoid(x)

def _layernorm(x, axis=-1, eps=1e-05):
    m = jnp.mean(x, axis=axis, keepdims=True)
    v = jnp.var(x, axis=axis, keepdims=True)
    return (x - m) / jnp.sqrt(v + eps)

def _scatter_add(tgt, idx, src, axis=0):
    return tgt.at[idx].add(src)

def _segment_sum(src, seg, n):
    return jax.ops.segment_sum(src, seg, n)
kernel_name = 'mk_flamingo_gated_d1_seqx_r8_6c934b'

def setup_inputs(seed: int=0):
    np.random.seed(seed)
    _w = jnp.asarray

    def _rec_inputs():
        import jax
        import jax.numpy as jnp
        _rk = jax.random.key(seed)
        x = -0.0002928 + 1 * jax.random.normal(jax.random.fold_in(_rk, 1), (16, 128, 256), jnp.float32)
        _lenS = 128 - jax.random.randint(jax.random.fold_in(_rk, 7), (16,), 0, max(1, 128 // 4) + 1, jnp.int32)
        _lenS2 = 128 - jax.random.randint(jax.random.fold_in(_rk, 8), (16,), 0, max(1, 128 // 4) + 1, jnp.int32)
        _ctx_2048P = jax.random.normal(jax.random.fold_in(_rk, 11), (16, 16, 256), jnp.float32)
        _ctx_2048c = jax.random.dirichlet(jax.random.fold_in(_rk, 511), 0.3 * jnp.ones((16,), jnp.float32), (16, 128))
        _ctx_2048t = jnp.einsum('bsk,bkd->bsd', _ctx_2048c, _ctx_2048P)
        _ctx_2048t = _ctx_2048t * jax.lax.rsqrt(jnp.mean(jnp.square(_ctx_2048t)) + 1e-12) * 0.953939
        ctx_2048 = -1.39393e-06 + 0.999914 * (_ctx_2048t + 0.3 * jax.random.normal(jax.random.fold_in(_rk, 611), (16, 128, 256), jnp.float32))
        _validS = jnp.arange(128)[None, :] < _lenS[:, None]
        _validS2 = jnp.arange(128)[None, :] < _lenS2[:, None]
        _causal = jnp.tril(jnp.ones((128, 128), dtype=bool))
        mask_Bx1x2048_fk1 = jnp.where(jnp.ones((16, 1, 256), dtype=bool), 1.0, 0.0).astype(jnp.float32)
        _g = jax.random.normal(jax.random.fold_in(_rk, 9001), (2, 1), jnp.float32)
        _g = jnp.sign(_g) * jnp.maximum(jnp.abs(_g), 1.0) + (_g == 0) * 1.0
        g_xattn = _g[0]
        g_ffn = _g[1]
        return (x, ctx_2048, mask_Bx1x2048_fk1, g_xattn, g_ffn)
    x, ctx_2048, mask_Bx1x2048_fk1, g_xattn, g_ffn = _rec_inputs()

    def _L0_xattn_setup():
        import math
        import jax, jax.numpy as jnp
        import numpy as np
        SIZE = 128
        HEADS = 16
        HEAD_DIM = SIZE // HEADS
        B, T, S = (2, 256, 256)
        NEG = 1000000.0
        key = jax.random.key(seed)
        ks = jax.random.split(key, 10)
        target = jax.random.normal(ks[0], (B, SIZE, T), dtype=jnp.float32)
        source = jax.random.normal(ks[1], (B, SIZE, S), dtype=jnp.float32)
        target_mask = (jax.random.uniform(ks[2], (B, 1, T)) > 0.1).astype(jnp.float32)
        source_mask = (jax.random.uniform(ks[3], (B, 1, S)) > 0.1).astype(jnp.float32)
        scale = 1.0 / math.sqrt(SIZE)
        Wq = jax.random.normal(ks[4], (SIZE, SIZE), dtype=jnp.float32) * scale
        Wk = jax.random.normal(ks[5], (SIZE, SIZE), dtype=jnp.float32) * scale
        Wv = jax.random.normal(ks[6], (SIZE, SIZE), dtype=jnp.float32) * scale
        bq = jax.random.normal(ks[7], (SIZE,), dtype=jnp.float32) * 0.01
        bk = jax.random.normal(ks[8], (SIZE,), dtype=jnp.float32) * 0.01
        bv = jax.random.normal(ks[9], (SIZE,), dtype=jnp.float32) * 0.01
        return {'target': target, 'source': source, 'target_mask': target_mask, 'source_mask': source_mask, 'Wq': Wq, 'bq': bq, 'Wk': Wk, 'bk': bk, 'Wv': Wv, 'bv': bv}
    _L0_xattn_all = _L0_xattn_setup()
    _L0_xattn_in = {k: v for k, v in _L0_xattn_all.items() if k in ('Wq', 'bq', 'Wk', 'bk', 'Wv', 'bv')}
    del _L0_xattn_all

    def _L0_ffn_setup():
        import jax, jax.numpy as jnp
        import numpy as np
        import math
        N_EMBD = 256
        N_HEAD = 16
        HEAD_DIM = N_EMBD // N_HEAD
        B, T = (2, 256)
        key = jax.random.key(seed)
        k1, k2, k3 = jax.random.split(key, 3)
        x = jax.random.normal(k1, (B, T, N_EMBD), dtype=jnp.float32)
        W_gate = jax.random.normal(k2, (N_HEAD, N_EMBD), dtype=jnp.float32) * 0.02
        W_qkv = jax.random.normal(k3, (3 * N_EMBD, N_EMBD), dtype=jnp.float32) * 0.02
        return {'x': x, 'W_gate': W_gate, 'W_qkv': W_qkv}
    _L0_ffn_all = _L0_ffn_setup()
    _L0_ffn_in = {k: v for k, v in _L0_ffn_all.items() if k in ('W_gate', 'W_qkv')}
    del _L0_ffn_all
    return {'x': x, 'ctx_2048': ctx_2048, 'mask_Bx1x2048_fk1': mask_Bx1x2048_fk1, 'g_xattn': g_xattn, 'g_ffn': g_ffn, 'L0_xattn_Wq': _L0_xattn_in['Wq'], 'L0_xattn_bq': _L0_xattn_in['bq'], 'L0_xattn_Wk': _L0_xattn_in['Wk'], 'L0_xattn_bk': _L0_xattn_in['bk'], 'L0_xattn_Wv': _L0_xattn_in['Wv'], 'L0_xattn_bv': _L0_xattn_in['bv'], 'L0_ffn_W_gate': _L0_ffn_in['W_gate'], 'L0_ffn_W_qkv': _L0_ffn_in['W_qkv']}

def reference(x, ctx_2048, mask_Bx1x2048_fk1, g_xattn, g_ffn, L0_xattn_Wq, L0_xattn_bq, L0_xattn_Wk, L0_xattn_bk, L0_xattn_Wv, L0_xattn_bv, L0_ffn_W_gate, L0_ffn_W_qkv):
    import jax
    import jax.numpy as jnp

    def _L0_xattn_ref(target, source, target_mask, source_mask, Wq, bq, Wk, bk, Wv, bv):
        import math
        import jax, jax.numpy as jnp
        import numpy as np
        SIZE = 128
        HEADS = 16
        HEAD_DIM = SIZE // HEADS
        B, T, S = (2, 256, 256)
        NEG = 1000000.0
        b, _, t = target.shape
        s = source.shape[-1]
        q = jnp.einsum('oc,bct->bot', Wq, target) + bq[None, :, None]
        k = jnp.einsum('oc,bcs->bos', Wk, source) + bk[None, :, None]
        v = jnp.einsum('oc,bcs->bos', Wv, source) + bv[None, :, None]
        q = q.reshape(b, HEADS, HEAD_DIM, t)
        k = k.reshape(b, HEADS, HEAD_DIM, s)
        v = v.reshape(b, HEADS, HEAD_DIM, s)
        dot = jnp.einsum('bhdt,bhds->bhts', q, k) / math.sqrt(HEAD_DIM)
        mask = target_mask[:, :, :, None] * source_mask[:, :, None, :]
        dot = mask * dot - (1.0 - mask) * NEG
        amap = jax.nn.softmax(dot, axis=-1) * mask
        out = jnp.einsum('bhts,bhds->bhdt', amap, v)
        return out.reshape(b, HEADS * HEAD_DIM, t)

    def _L0_ffn_ref(x, W_gate, W_qkv):
        import jax, jax.numpy as jnp
        import numpy as np
        import math
        N_EMBD = 256
        N_HEAD = 16
        HEAD_DIM = N_EMBD // N_HEAD
        B, T = (2, 256)
        Bb, Tt, C = x.shape
        H, hd = (N_HEAD, HEAD_DIM)
        gating = jax.nn.softmax(x @ W_gate.T, axis=-1)
        idx = jnp.argmax(gating, axis=-1)
        indicator = jax.nn.one_hot(idx, H, dtype=gating.dtype)
        top1_val = jnp.max(gating, axis=-1, keepdims=True)
        gating_top1 = indicator * top1_val
        qkv = x @ W_qkv.T
        q, k, v = jnp.split(qkv, 3, axis=-1)
        k = k.reshape(Bb, Tt, H, hd)
        v = v.reshape(Bb, Tt, H, hd)
        k_shared = jnp.einsum('bth,bthd->btd', indicator, k)
        v_shared = jnp.einsum('bth,bthd->btd', gating_top1, v)
        q = q.reshape(Bb, Tt, H, hd).transpose(0, 2, 1, 3)
        att = jnp.einsum('bhqd,bkd->bhqk', q, k_shared) * (1.0 / math.sqrt(hd))
        causal = jnp.tril(jnp.ones((Tt, Tt), dtype=bool))
        att = jnp.where(causal[None, None, :, :], att, -jnp.inf)
        att = jax.nn.softmax(att, axis=-1)
        y = jnp.einsum('bhqk,bkd->bhqd', att, v_shared)
        y = y.transpose(0, 2, 1, 3).reshape(Bb, Tt, C)
        return y
    x = x + jnp.tanh(g_xattn[0]) * _L0_xattn_ref(_layernorm(x, axis=-1), ctx_2048, mask_Bx1x2048_fk1, mask_Bx1x2048_fk1, L0_xattn_Wq, L0_xattn_bq, L0_xattn_Wk, L0_xattn_bk, L0_xattn_Wv, L0_xattn_bv)
    x = x + jnp.tanh(g_ffn[0]) * _L0_ffn_ref(_layernorm(x, axis=-1), L0_ffn_W_gate, L0_ffn_W_qkv)
    return x

_drawn_inputs = setup_inputs


def setup_inputs(seed=0):
    import zlib

    import numpy as np

    out = dict(_drawn_inputs(seed))
    spreads = {}
    factors = {'L0_xattn_bq': 21.553,
     'L0_xattn_bk': 64.0,
     'L0_xattn_bv': 6.846,
     'L0_ffn_W_gate': 4.75,
     'L0_ffn_W_qkv': 3.78}
    for name, (base, spread) in spreads.items():
        noise = np.random.default_rng([zlib.crc32(name.encode()), seed]).standard_normal(out[name].shape)
        drawn = base * np.exp(spread * noise) if base else spread * noise
        out[name] = jnp.asarray(drawn.astype(out[name].dtype))
    for name, factor in factors.items():
        out[name] = (out[name] * factor).astype(out[name].dtype)
    return out
```

```python
from contextlib import ExitStack

import concourse.bass as bass
from concourse import mybir

F32 = mybir.dt.float32
BF16 = mybir.dt.bfloat16
ALU = mybir.AluOpType
ACT = mybir.ActivationFunctionType
AX = mybir.AxisListType

P = 128
LEVELS = 3
BANK = 512
EPS = 1e-5
NEG = 1000000.0

PAIRS = [(0, 0), (1, 0), (2, 0), (0, 1), (1, 1), (0, 2)]
Q_RUNS = [(0, 0, 3), (3, 0, 2), (5, 0, 1)]
K_RUNS = [(n, k, 1) for n, (q, k) in enumerate(PAIRS)]
MAX_ROW = 96
ROWS = MAX_ROW + LEVELS
V_RING = 4
DMA = 16


class Batch:

    def __init__(self, c, k=None, m=0):
        self.c, self.k, self.m = c, k, m

    def __add__(self, n):
        return Batch(self.c + n, self.k, self.m)

    def times(self, f, extra=0):
        return f * self.c + extra if self.k is None else self.k * (f * self.m) + (f * self.c + extra)

    def uses(self, f, extra=0, ring=2):
        n = f * (self.c // ring) + extra
        return n if self.k is None else self.k * (f * self.m // ring) + n

    @property
    def index(self):
        return self.times(1)

    @property
    def least(self):
        return self.c

    def slot(self, ring=2):
        return self.c % ring


def reached(eng, semaphore, b, per_batch, extra=0):
    first = per_batch * b.c + extra
    if b.k is None:
        if first > 0:
            eng.wait_ge(semaphore, first)
    else:
        assert first >= 0
        eng.wait_ge(semaphore, b.times(per_batch, extra))


def wait_apart(eng, held, *waits):
    values = [(semaphore, v if isinstance(v, int) else eng.to_reg(v)) for semaphore, v in waits]
    eng.wait_ge(*held)
    for semaphore, v in values:
        if not isinstance(v, int) or v > 0:
            eng.wait_ge(semaphore, v)


class Chain:

    def __init__(self, eng, sem):
        self.eng, self.sem, self.base, self.n = eng, sem, 0, 0

    def __call__(self, instruction):
        instruction.then_inc(self.sem, 1)
        self.n += 1
        self.eng.wait_ge(self.sem, self.base + self.n)

    def enter(self, k, per_turn):
        self.start = self.base + self.n
        self.base, self.n, self.per_turn = k * per_turn + self.start, 0, per_turn

    def leave(self, turns):
        assert self.n == self.per_turn, (self.n, self.per_turn)
        self.base, self.n = self.start + turns * self.per_turn, 0


def flamingo_kernel(nc, x, ctx_in, mask, g_xattn, g_ffn, Wq, bq, Wk, bk, Wv, bv, W_gate, W_qkv, out):
    B, T, C = x.shape
    H = W_gate.shape[0]
    DX = T // H
    DF = C // H
    PT = C // P
    GROUPS = 4
    CHX = DX + 1
    PAIR_ROWS_X = len(PAIRS) * CHX
    assert T == P and C == PT * P and PAIR_ROWS_X <= MAX_ROW and len(PAIRS) * DF == MAX_ROW
    assert P // GROUPS >= 2 * DX + 2 and H == GROUPS * GROUPS
    HALF = H // 2
    XATTN_SCALE = float(DX) ** -0.5
    FFN_SCALE = float(DF) ** -0.5

    q_levels = nc.dram_tensor("q_levels", (B, LEVELS, CHX, H, C), BF16).ap()
    k_levels = nc.dram_tensor("k_levels", (B, LEVELS, CHX, H, C), BF16).ap()
    qf_levels = nc.dram_tensor("qf_levels", (B, LEVELS, DF, H, T), BF16).ap()

    with ExitStack() as stack:
        def sb(name, shape, dt=F32):
            return stack.enter_context(nc.sbuf_tensor(name, shape, dt))

        def sem(name):
            return stack.enter_context(nc.semaphore(name))

        psum = stack.enter_context(nc.psum_tensor("psum", [P, 8, BANK], F32))
        bank_max = [0, 1]
        bank_exp = [2, 3]
        BANK_PV, BANK_A, BANK_B, BANK_C = 4, 5, 6, 7

        ident = sb("ident", [P, P])
        ident_bf = sb("ident_bf", [P, P], BF16)
        causal_bf = sb("causal_bf", [P, P], BF16)
        ones_row = sb("ones_row", [1, P])
        half_power = sb("half_power", [P, 1])
        first_head = sb("first_head", [P, H])
        w_rows = sb("w_rows", [P, 3, P])
        wqkv_rows = sb("wqkv_rows", [P, 3 * C // P, C])
        wgate_rows = sb("wgate_rows", [H, C])
        wT = sb("wT", [P, 3, P])
        bias_rows = sb("bias_rows", [1, 2, P])
        bias_perm = sb("bias_perm", [1, 2, P])
        bias_col = sb("bias_col", [P, 2])
        bv_all = sb("bv_all", [P, P])
        gates_in = sb("gates_in", [P, 2])
        gates = sb("gates", [P, 2])
        mask_rows = sb("mask_rows", [B * PT, P])
        mask_col = sb("mask_col", [P, B * PT])
        mask_gate = sb("mask_gate", [P, B * PT])
        mask_b = sb("mask_b", [B, C])
        aug_f = sb("aug_f", [B, 2, C])
        aug_r = sb("aug_r", [B, 2, C])
        aug_levels = sb("aug_levels", [B, 2, LEVELS, C], BF16)
        wfT = sb("wfT", [P, PT, 3 * C])
        wgT = sb("wgT", [P, PT, H])

        xs = sb("xs", [P, B, C])
        ctx = sb("ctx", [P, 2, C])
        mask_all = sb("mask_all", [P, 2, C])
        stats = sb("stats", [P, 6])
        meanvar = sb("meanvar", [P, 2])
        rstd = sb("rstd", [P, 2])
        xn = sb("xn", [P, C])
        qk_raw = sb("qk_raw", [P, 2, C])
        qk_f = sb("qk_f", [P, 2, C])
        qk_rest = sb("qk_rest", [P, 2, C])
        qk_levels = sb("qk_levels", [P, 2, LEVELS, C], BF16)
        v_sum = sb("v_sum", [P, PT, P])
        v_cols = sb("v_cols", [P, V_RING, PT, H, 32])
        q_stack = sb("q_stack", [P, 2, H, C], BF16)
        k_stack = sb("k_stack", [P, 2, H, C], BF16)
        neg_max = sb("neg_max", [P, H, PT])
        max_rest = sb("max_rest", [P, HALF * PT])
        max_levels = sb("max_levels", [P, P], BF16)
        max_rows = sb("max_rows", [LEVELS * HALF * PT, 2, P], BF16)
        probs = sb("probs", [P, 4, GROUPS, PT * C])
        pv_out = sb("pv_out", [P, 2 * C])
        recip = sb("recip", [P, 32])
        recip_g = sb("recip_g", [P, 32])
        attn_t = sb("attn_t", [P, PT, P])

        stats_f = sb("stats_f", [P, 6])
        meanvar_f = sb("meanvar_f", [P, 2])
        rstd_f = sb("rstd_f", [P, 2])
        xn_f = sb("xn_f", [P, C])
        xnT = sb("xnT", [P, PT, T])
        qf_f = sb("qf_f", [P, PT * T])
        qf_rest = sb("qf_rest", [P, PT * T])
        qf_lev = sb("qf_lev", [P, LEVELS, PT * T], BF16)
        logit = sb("logit", [P, H])
        top_neg = sb("top_neg", [P, 2])
        gate_e = sb("gate_e", [P, H])
        gate_sum = sb("gate_sum", [P, 2])
        rank = sb("rank", [P, H])
        rank_top = sb("rank_top", [P, 1])
        chosen = sb("chosen", [P, H])
        kv_sel = sb("kv_sel", [P, 2, H, DF])
        kv_one = sb("kv_one", [P, 2, DF])
        kf_rest = sb("kf_rest", [P, 2, DF])
        kf_rows = sb("kf_rows", [P, ROWS], BF16)
        vf_cols = sb("vf_cols", [P, V_RING, P // GROUPS])
        kf_stack = sb("kf_stack", [ROWS, 4, T], BF16)
        qf_stack = sb("qf_stack", [ROWS, 2, H, T], BF16)
        neg_max_f = sb("neg_max_f", [P, H])
        maxf_rest = sb("maxf_rest", [P, H])
        maxf_levels = sb("maxf_levels", [P, LEVELS * HALF], BF16)
        maxf_rows = sb("maxf_rows", [LEVELS * HALF, 2, P], BF16)
        probs_f = sb("probs_f", [P, 2, H * T])
        pvf_out = sb("pvf_out", [P, BANK])
        recip_f = sb("recip_f", [P, H])
        recip_fg = sb("recip_fg", [P, H])
        y_f = sb("y_f", [P, C])
        out_sb = sb("out_sb", [P, 2, C])

        S = {}
        for name in (
            "weights_in small_in x_first x_rest mask_in qkv_in "
            "ident_zero const_ready pool_chain dve_chain act_chain memset_done w_transposed w_copied wf_transposed wf_copied "
            "bias_ordered bias_mm bias_copied tanh_done aug_ready maskT_mm maskcol_ready aug_written vcols_ready "
            "norm_stats rstd_ready xn_ready qk_mm v_mm qk_copied v_added qk_masked qk_high qk_resid qk_mid qk_low v_ready "
            "scores_max max_taken max_split maxT_mm maxT_copied scores_exp exp_done pv_done pv_copied "
            "outT_mm attn_normed attnT_mm x_updated "
            "f_stats f_rstd f_xn f_xnT_mm f_xnT f_kv_mm f_gq_mm f_logit f_gate_e f_selected f_q_copied f_q_high f_q_resid f_q_mid "
            "f_q_low f_kT_in f_kT_mm f_kT f_v_ready f_scores_max f_max_taken f_max_split f_maxT_mm f_maxT_copied f_scores_exp "
            "f_exp_done f_masked f_pv_done f_pv_copied f_outT_mm f_y_ready f_out_ready"
        ).split():
            S[name] = sem(name)
        in_loaded = [sem(f"in_loaded{i}") for i in range(2)]
        levels_out = [sem(f"levels_out{i}") for i in range(2)]
        stack_in = [[sem(f"stack_in{h}{i}") for i in range(2)] for h in range(2)]
        max_in = [[sem(f"max_in{h}{i}") for i in range(2)] for h in range(2)]
        f_levels_out = [sem(f"f_levels_out{i}") for i in range(2)]
        f_stack_in = [[sem(f"f_stack_in{h}{i}") for i in range(2)] for h in range(2)]
        f_max_in = [[sem(f"f_max_in{h}{i}") for i in range(2)] for h in range(2)]
        out_written = [sem(f"out_written{i}") for i in range(2)]
        STACK_DMAS = len(Q_RUNS) + len(K_RUNS)

        def schedule(eng, step, chain=None, per_step=0):
            unroll = V_RING
            turns = (B - 4) // unroll
            assert turns * unroll == B - 4
            for s in range(-3, 1):
                step(Batch(s))
            with eng.Fori(0, turns) as k:
                if chain:
                    chain.enter(k, per_step * unroll)
                for u in range(unroll):
                    step(Batch(1 + u, k, unroll))
            if chain:
                chain.leave(turns)
            for s in range(B - 3, B + 1):
                step(Batch(s))

        def live(b):
            return b.k is not None or 0 <= b.c < B

        block = stack.enter_context(nc.Block())

        @block.sync
        def _(sp):
            for n, w in enumerate((Wq, Wk, Wv)):
                sp.dma_start(w_rows[:, n, :], w).then_inc(S["weights_in"], DMA)
            sp.dma_start(xs[:, 0:4, :], x[0:4].rearrange("b t c -> t b c")).then_inc(S["x_first"], DMA)
            for n, v in enumerate((bq, bk)):
                sp.dma_start(bias_rows[:, n, :], v.rearrange("(a n) -> a n", a=1)).then_inc(S["small_in"], DMA)
            sp.dma_start(bv_all[:, :], bv.rearrange("(a n) -> a n", a=1).to_broadcast([P, P])).then_inc(S["small_in"], DMA)
            for n, v in enumerate((g_xattn, g_ffn)):
                sp.dma_start(gates_in[:, n:n + 1], v.rearrange("(a n) -> a n", a=1).to_broadcast([P, 1]))\
                    .then_inc(S["small_in"], DMA)
            sp.dma_start(mask_rows[:, :], mask.rearrange("b a (t p) -> (b a t) p", p=P)).then_inc(S["mask_in"], DMA)
            sp.dma_start(mask_b[:, :], mask.rearrange("b a c -> (b a) c")).then_inc(S["mask_in"], DMA)

            sp.wait_ge(S["aug_ready"], 1)
            for side, levels in enumerate((q_levels, k_levels)):
                for l in range(LEVELS):
                    sp.dma_start(levels[:, l, DX],
                                 aug_levels[:, side, l, :].unsqueeze(1).to_broadcast([B, H, C]))\
                        .then_inc(S["aug_written"], DMA)

            loaded = (S["weights_in"], 3 * DMA)

            def load_inputs(b):
                if not live(b):
                    return
                wait_apart(sp, loaded, (S["v_mm"], b.times(1, -1)), (S["qk_masked"], b.times(1, -1)))
                sp.dma_start(ctx[:, b.slot(), :], ctx_in[b.index]).then_inc(in_loaded[b.slot()], DMA)
                sp.dma_start(mask_all[:, b.slot(), :], mask[b.index].to_broadcast([P, C]))\
                    .then_inc(in_loaded[b.slot()], DMA)

            def write_levels(b):
                if not live(b):
                    return
                wait_apart(sp, loaded, (S["qk_low"], b.times(1, 1)))
                for side, levels in enumerate((q_levels, k_levels)):
                    sp.dma_start(levels[b.index][:, 0:DX].rearrange("l d h c -> (d h) l c"),
                                 qk_levels[:, side]).then_inc(levels_out[b.slot()], DMA)

            def load_stack(b, half):
                if not live(b):
                    return
                h0 = half * HALF
                wait_apart(sp, loaded, (levels_out[b.slot()], b.uses(2 * DMA, 2 * DMA)),
                           (S["aug_written"], 2 * LEVELS * DMA),
                           (S["scores_exp"], b.times(H, (half + 1) * HALF - 2 * H)))
                if b.k is None and b.c < 2:
                    sp.wait_ge(S["memset_done"], 3 * (b.c + 1))
                for dst, src, runs in ((q_stack, q_levels, Q_RUNS), (k_stack, k_levels, K_RUNS)):
                    for pair, level, n in runs:
                        sp.dma_start(dst[pair * CHX:(pair + n) * CHX, b.slot(), h0:h0 + HALF, :],
                                     src[b.index][level:level + n, :, h0:h0 + HALF, :]
                                     .rearrange("l d h c -> (l d) h c"))\
                            .then_inc(stack_in[half][b.slot()], DMA)

            def load_max(b, half):
                if not live(b):
                    return
                wait_apart(sp, loaded, (S["maxT_copied"], b.times(2, half + 1)),
                           (S["scores_exp"], b.times(H, (half + 1) * HALF - 2 * H)))
                n = HALF * PT
                for l in range(LEVELS):
                    sp.dma_start(q_stack[MAX_ROW + l:MAX_ROW + l + 1, b.slot(), half * HALF:(half + 1) * HALF, :]
                                 .rearrange("a h (t p) -> a (h t) p", p=P),
                                 max_rows[l * n:(l + 1) * n, half, :])\
                        .then_inc(max_in[half][b.slot()], DMA)

            def cross_step(s):
                load_inputs(s + 3)
                if s.k is None and s.c == -3:
                    sp.dma_start(xs[:, 4:B, :], x[4:B].rearrange("b t c -> t b c")).then_inc(S["x_rest"], DMA)
                    sp.dma_start(wqkv_rows[:, :, :], W_qkv.rearrange("(n p) c -> p n c", p=P)).then_inc(S["qkv_in"], DMA)
                    sp.dma_start(wgate_rows[:, :], W_gate).then_inc(S["qkv_in"], DMA)
                load_max(s, 1)
                load_stack(s + 2, 0)
                load_max(s + 1, 0)
                write_levels(s + 3)
                load_stack(s + 2, 1)

            schedule(sp, cross_step)

            def write_f_levels(b):
                if not live(b):
                    return
                wait_apart(sp, loaded, (S["f_q_low"], b.times(1, 1)))
                for t in range(PT):
                    n = DF // PT
                    sp.dma_start(qf_levels[b.index][:, t * n:(t + 1) * n].rearrange("l d h c -> (d h) l c"),
                                 qf_lev[:, :, t * T:(t + 1) * T]).then_inc(f_levels_out[b.slot()], DMA)

            def load_f_stack(b, half):
                if not live(b):
                    return
                wait_apart(sp, loaded, (f_levels_out[b.slot()], b.uses(PT * DMA, PT * DMA)),
                           (S["f_scores_exp"], b.times(4, 2 * (half + 1) - 8)))
                h0 = half * HALF
                for pair, level, n in Q_RUNS:
                    sp.dma_start(qf_stack[pair * DF:(pair + n) * DF, b.slot(), h0:h0 + HALF, :],
                                 qf_levels[b.index][level:level + n, :, h0:h0 + HALF, :]
                                 .rearrange("l d h c -> (l d) h c")).then_inc(f_stack_in[half][b.slot()], DMA)

            def load_f_max(b, half):
                if not live(b):
                    return
                wait_apart(sp, loaded, (S["f_maxT_copied"], b.times(2, half + 1)),
                           (S["f_scores_exp"], b.times(4, 2 * (half + 1) - 8)))
                for l in range(LEVELS):
                    sp.dma_start(qf_stack[MAX_ROW + l:MAX_ROW + l + 1, b.slot(), half * HALF:(half + 1) * HALF, :],
                                 maxf_rows[l * HALF:(l + 1) * HALF, half, :])\
                        .then_inc(f_max_in[half][b.slot()], DMA)

            def store(b):
                if not live(b):
                    return
                wait_apart(sp, loaded, (S["f_out_ready"], b.times(1, 1)))
                sp.dma_start(out[b.index], out_sb[:, b.slot(), :]).then_inc(out_written[b.slot()], DMA)

            def causal_step(s):
                load_f_max(s, 1)
                write_f_levels(s + 2)
                load_f_stack(s + 2, 0)
                load_f_max(s + 1, 0)
                store(s + -1)
                load_f_stack(s + 2, 1)

            schedule(sp, causal_step)
            for i in range(2):
                sp.wait_ge(out_written[i], B // 2 * DMA)
                sp.wait_ge(levels_out[i], B // 2 * 2 * DMA)
                sp.wait_ge(f_levels_out[i], B // 2 * PT * DMA)
            sp.wait_ge(S["aug_written"], 2 * LEVELS * DMA)

        @block.gpsimd
        def _(pool):
            chain = Chain(pool, S["pool_chain"])
            chain(nc.gpsimd.memset(ident[:, :], 0.0))
            chain(nc.gpsimd.affine_select(out=ident[:, :], in_=ident[:, :], compare_op=ALU.not_equal, fill=1.0, base=0,
                                          pattern=[[-1, P]], channel_multiplier=1))
            nc.gpsimd.tensor_copy(ident_bf[:, :], ident[:, :]).then_inc(S["const_ready"], 1)
            nc.gpsimd.memset(ones_row[:, :], 1.0).then_inc(S["const_ready"], 1)
            chain(nc.gpsimd.memset(half_power[:, :], -0.5))
            chain(nc.gpsimd.memset(v_cols[:, :, :, :, :], 0.0))
            for n in range(V_RING):
                for slot in range(2):
                    view = v_cols[:, n, :, :, :].rearrange("p t (r s j) x -> p (t r) s j x", s=2, j=GROUPS)
                    last = nc.gpsimd.memset(view[:, :, slot, :, 2 * DX + slot:2 * DX + slot + 1], 1.0)
                    last.then_inc(S["vcols_ready"], 1)
            pool.wait_ge(S["vcols_ready"], 2 * V_RING)
            chain(nc.gpsimd.memset(causal_bf[:, :], 0.0))
            chain(nc.gpsimd.affine_select(out=causal_bf[:, :], in_=causal_bf[:, :], compare_op=ALU.is_ge, fill=-1e30,
                                          base=0, pattern=[[-1, P]], channel_multiplier=1))
            chain(nc.gpsimd.memset(vf_cols[:, :, :], 0.0))
            nc.gpsimd.memset(vf_cols[:, :, DF:DF + 1], 1.0).then_inc(S["const_ready"], 1)
            for h in range(H):
                last = nc.gpsimd.memset(first_head[:, h:h + 1], float(H - h))
            chain(last)
            chain(nc.gpsimd.memset(kf_rows[:, :], 1.0))
            chain(nc.gpsimd.memset(max_levels[:, :], 0.0))

            def inverse_std(r, ready, signal, b):
                pool.wait_ge(ready, b.times(1, 1))
                nc.gpsimd.tensor_tensor(r[:, 1:2], r[:, 0:1], half_power[:, :], ALU.pow).then_inc(signal, 1)

            def cross_step(s):
                bp = s + 3
                if live(bp):
                    inverse_std(rstd, S["norm_stats"], S["rstd_ready"], bp)
                    pool.wait_ge(S["qk_copied"], bp.times(1, 1))
                    pool.wait_ge(in_loaded[bp.slot()], bp.uses(2 * DMA, 2 * DMA))
                    nc.gpsimd.tensor_tensor(qk_f[:, :, :], qk_raw[:, :, :],
                                            mask_all[:, bp.slot(), :].unsqueeze(1).to_broadcast([P, 2, C]),
                                            ALU.mult).then_inc(S["qk_masked"], 1)
                    pool.wait_ge(S["qk_high"], bp.times(1, 1))
                    nc.gpsimd.tensor_tensor(qk_rest[:, :, :], qk_f[:, :, :], qk_levels[:, :, 0, :], ALU.subtract)\
                        .then_inc(S["qk_resid"], 1)
                    pool.wait_ge(S["v_added"], bp.times(1, 1))
                    if bp.k is None and bp.c == 0:
                        pool.wait_ge(S["maskcol_ready"], 1)
                    reached(pool, S["pv_done"], bp, 4, -12)
                    for t in range(PT):
                        for slot in range(2):
                            dst = v_cols[:, bp.slot(V_RING), t, :, :].rearrange("p (r s j) x -> p r s j x", s=2, j=GROUPS)
                            src = v_sum[:, t, :].rearrange("p (r s j d) -> p r s j d", s=2, j=GROUPS, d=DX)
                            col = mask_col[:, bass.ds(bp.times(PT, t), 1)]
                            last = nc.gpsimd.tensor_tensor(
                                dst[:, :, slot, :, slot * DX:(slot + 1) * DX], src[:, :, slot, :, :],
                                col.unsqueeze(2).unsqueeze(3).to_broadcast([P, 2, GROUPS, DX]), ALU.mult)
                    last.then_inc(S["v_ready"], 1)
                    pool.wait_ge(S["qk_mid"], bp.times(1, 1))
                    nc.gpsimd.tensor_tensor(qk_levels[:, :, 2, :], qk_rest[:, :, :], qk_levels[:, :, 1, :], ALU.subtract)\
                        .then_inc(S["qk_low"], 1)

            schedule(pool, cross_step)

            def causal_step(s):
                nxt2, new = s + 2, s + 3
                if live(new):
                    inverse_std(rstd_f, S["f_stats"], S["f_rstd"], new)
                if live(nxt2):
                    pool.wait_ge(S["f_q_high"], nxt2.times(1, 1))
                    nc.gpsimd.tensor_tensor(qf_rest[:, :], qf_f[:, :], qf_lev[:, 0, :], ALU.subtract)\
                        .then_inc(S["f_q_resid"], 1)
                for n in range(4):
                    if live(s):
                        wait_apart(pool, (S["const_ready"], 3), (S["f_exp_done"], s.times(4, n + 1)))
                        part = probs_f[:, s.slot(), n * BANK:(n + 1) * BANK]
                        nc.gpsimd.affine_select(out=part, in_=part, compare_op=ALU.is_ge, fill=0.0, base=0,
                                                pattern=[[0, GROUPS], [1, T]], channel_multiplier=-1)\
                            .then_inc(S["f_masked"], 1)
                    if n == 0 and live(nxt2):
                        pool.wait_ge(S["f_q_mid"], nxt2.times(1, 1))
                        nc.gpsimd.tensor_tensor(qf_lev[:, 2, :], qf_rest[:, :], qf_lev[:, 1, :], ALU.subtract)\
                            .then_inc(S["f_q_low"], 1)

            schedule(pool, causal_step)

        @block.tensor
        def _(pe):
            mm = nc.tensor.matmul

            pe.wait_ge(S["weights_in"], 3 * DMA)
            pe.wait_ge(S["const_ready"], 2)
            pe.wait_ge(S["pool_chain"], 2)
            for n in range(3):
                last = nc.tensor.transpose(psum[:, BANK_A, n * P:(n + 1) * P], w_rows[:, n, :], ident[:, :])
            last.then_inc(S["w_transposed"], 1)
            pe.wait_ge(S["bias_ordered"], 2)
            for n in range(2):
                last = mm(psum[:, BANK_B, n:n + 1],
                          bias_perm[0:1, n, :], ones_row[0:1, 0:1],
                          start=True, stop=True)
            last.then_inc(S["bias_mm"], 1)
            pe.wait_ge(S["mask_in"], 2 * DMA)
            nc.tensor.transpose(psum[:, BANK_C, 0:B * PT], mask_rows[:, :], ident[0:B * PT, 0:B * PT])\
                .then_inc(S["maskT_mm"], 1)
            pe.wait_ge(S["w_copied"], 3)
            pe.wait_ge(S["bias_copied"], 2)

            def project_qk(b):
                pe.wait_ge(S["xn_ready"], b.times(1, 1))
                pe.wait_ge(in_loaded[b.slot()], b.uses(2 * DMA, 2 * DMA))
                reached(pe, S["qk_copied"], b, 1)
                reached(pe, S["attn_normed"], b, 1, -4)
                mm(psum[:, BANK_A, 0:C], wT[:, 0, :], xn[:, :], start=True, stop=True)
                mm(psum[:, BANK_A, C:2 * C], wT[:, 1, :], ctx[:, b.slot(), :], start=True, stop=True)\
                    .then_inc(S["qk_mm"], 1)

            def project_v(b):
                reached(pe, S["v_added"], b, 1)
                reached(pe, S["maxT_copied"], b, 2, -4)
                for t in range(PT):
                    last = mm(psum[:, BANK_B, t * P:(t + 1) * P], ctx[:, b.slot(), t * P:(t + 1) * P], wT[:, 2, :],
                              start=True, stop=True)
                last.then_inc(S["v_mm"], 1)

            def max_scores(b, h):
                if h % HALF == 0:
                    pe.wait_ge(stack_in[h // HALF][b.slot()], b.uses(STACK_DMAS * DMA, STACK_DMAS * DMA))
                reached(pe, S["max_taken"], b, H, h - 1)
                for t in range(PT):
                    last = mm(psum[:, bank_max[h % 2], t * C:(t + 1) * C],
                              q_stack[0:MAX_ROW, b.slot(), h, t * P:(t + 1) * P],
                              k_stack[0:MAX_ROW, b.slot(), h, :], start=True, stop=True)
                last.then_inc(S["scores_max"], 1)

            def turn_max(b, half):
                pe.wait_ge(S["max_split"], b.times(2, half + 1))
                nc.tensor.transpose(psum[:, BANK_B, 0:P // 2].bitcast(BF16), max_levels[:, :], ident_bf[:, :])\
                    .then_inc(S["maxT_mm"], 1)

            def exp_scores(b, h):
                if h % HALF == 0:
                    pe.wait_ge(max_in[h // HALF][b.slot()], b.uses(LEVELS * DMA, LEVELS * DMA))
                reached(pe, S["exp_done"], b, H, h - 1)
                for t in range(PT):
                    last = mm(psum[:, bank_exp[h % 2], t * C:(t + 1) * C],
                              k_stack[0:ROWS, b.slot(), h, t * P:(t + 1) * P],
                              q_stack[0:ROWS, b.slot(), h, :], start=True, stop=True)
                last.then_inc(S["scores_exp"], 1)

            def value_product(b, quad, t):
                region = quad // 2
                if t == 0:
                    pe.wait_ge(S["exp_done"], b.times(H, GROUPS * (quad + 1)))
                    if quad == 0:
                        pe.wait_ge(S["v_ready"], b.times(1, 1))
                        reached(pe, S["pv_copied"], b, 1)
                for j in range(GROUPS):
                    last = mm(psum[j * 32:(j + 1) * 32, BANK_PV, region * C:(region + 1) * C],
                              v_cols[:, b.slot(V_RING), t, GROUPS * quad + j, :],
                              probs[:, quad, j, t * C:(t + 1) * C],
                              start=(quad % 2 == 0 and t == 0), stop=(quad % 2 == 1 and t == PT - 1),
                              skip_group_check=True)
                if t == PT - 1:
                    last.then_inc(S["pv_done"], 1)

            def turn_outputs(b):
                pe.wait_ge(S["pv_copied"], b.times(1, 1))
                for t in range(PT):
                    for r in range(2):
                        n = t * 2 + r
                        last = nc.tensor.transpose(psum[:, BANK_A, n * P:(n + 1) * P],
                                                   pv_out[:, r * C + t * P:r * C + (t + 1) * P], ident[:, :])
                last.then_inc(S["outT_mm"], 1)

            def turn_back(b):
                pe.wait_ge(S["attn_normed"], b.times(1, 1))
                reached(pe, S["x_updated"], b, 1)
                for t in range(PT):
                    last = nc.tensor.transpose(psum[:, BANK_B, t * P:(t + 1) * P], attn_t[:, t, :], ident[:, :])
                last.then_inc(S["attnT_mm"], 1)

            def turn_ffn_weights():
                pe.wait_ge(S["qkv_in"], 2 * DMA)
                for part, bank in enumerate((bank_exp[0], bank_exp[1], BANK_PV)):
                    for c in range(PT):
                        for t in range(PT):
                            last = nc.tensor.transpose(psum[:, bank, c * C + t * P:c * C + (t + 1) * P],
                                                       wqkv_rows[:, part * PT + t, c * P:(c + 1) * P], ident[:, :])
                for c in range(PT):
                    last = nc.tensor.transpose(psum[:, BANK_C, c * H:(c + 1) * H],
                                               wgate_rows[:, c * P:(c + 1) * P], ident[0:H, 0:H])
                last.then_inc(S["wf_transposed"], 1)

            def cross_step(s):
                before, nxt, new = s + -1, s + 1, s + 3
                if s.k is None and s.c == -1:
                    pe.wait_ge(S["maskcol_ready"], 1)
                    turn_ffn_weights()
                if s.k is None and s.c == 0:
                    pe.wait_ge(S["wf_copied"], 5)
                for h in range(H):
                    quad, j = divmod(h, GROUPS)
                    if live(nxt):
                        max_scores(nxt, h)
                    if live(s):
                        exp_scores(s, h)
                    if j % 2:
                        b, q = (before, GROUPS - 1) if quad == 0 else (s, quad - 1)
                        if live(b):
                            value_product(b, q, j // 2)
                    if h == 2 and live(s):
                        reached(pe, S["x_updated"], s, 1, -1)
                        turn_max(s, 1)
                    if h == 4 and live(new):
                        project_qk(new)
                    if h == 7 and live(new):
                        project_v(new)
                    if h == 9 and live(before):
                        if live(new):
                            pe.wait_ge(S["qk_copied"], new.times(1, 1))
                        reached(pe, S["attn_normed"], before, 1)
                        turn_outputs(before)
                    if h == 11 and live(nxt):
                        if live(new):
                            pe.wait_ge(S["v_added"], new.times(1, 1))
                        if live(s):
                            pe.wait_ge(S["maxT_copied"], s.times(2, 2))
                        turn_max(nxt, 0)
                    if h == 13 and live(before):
                        if live(nxt):
                            pe.wait_ge(S["maxT_copied"], nxt.times(2, 1))
                        elif live(s):
                            pe.wait_ge(S["maxT_copied"], s.times(2, 2))
                        turn_back(before)

            schedule(pe, cross_step)

            pe.wait_ge(S["max_taken"], H * B)
            pe.wait_ge(S["exp_done"], H * B)
            pe.wait_ge(S["x_updated"], B)
            pe.wait_ge(S["pv_copied"], B)
            pe.wait_ge(S["pool_chain"], 10)

            def f_turn_x(b):
                pe.wait_ge(S["f_xn"], b.times(1, 1))
                for c in range(PT):
                    last = nc.tensor.transpose(psum[:, BANK_B, c * T:(c + 1) * T], xn_f[:, c * P:(c + 1) * P], ident[:, :])
                last.then_inc(S["f_xnT_mm"], 1)

            def f_project_kv(b):
                reached(pe, S["f_selected"], b, 1)
                for c in range(PT):
                    last = mm(psum[:, BANK_A, :], xnT[:, c, :], wfT[:, c, C:3 * C], start=(c == 0), stop=(c == PT - 1))
                last.then_inc(S["f_kv_mm"], 1)

            def f_project_gq(b):
                pe.wait_ge(S["f_xnT"], b.times(1, 1))
                reached(pe, S["f_q_copied"], b, 1)
                for c in range(PT):
                    mm(psum[:, BANK_C, PT * T:PT * T + H], xnT[:, c, :], wgT[:, c, :], start=(c == 0), stop=(c == PT - 1))
                for t in range(PT):
                    for c in range(PT):
                        last = mm(psum[:, BANK_C, t * T:(t + 1) * T], wfT[:, c, t * P:(t + 1) * P], xnT[:, c, :],
                                  start=(c == 0), stop=(c == PT - 1))
                last.then_inc(S["f_gq_mm"], 1)

            def f_turn_k(b):
                pe.wait_ge(S["f_kT_in"], b.times(1, 1))
                nc.tensor.transpose(psum[0:ROWS, BANK_B, 0:T // 2].bitcast(BF16), kf_rows[:, :], ident_bf[:, :])\
                    .then_inc(S["f_kT_mm"], 1)

            def f_max_scores(b, n):
                if n == 0:
                    pe.wait_ge(S["f_kT"], b.times(1, 1))
                if n % 2 == 0:
                    pe.wait_ge(f_stack_in[n // 2][b.slot()], b.uses(len(Q_RUNS) * DMA, len(Q_RUNS) * DMA))
                reached(pe, S["f_max_taken"], b, 4, n - 1)
                bank = bank_max[n % 2]
                mm(psum[:, bank, :].rearrange("p (h t) -> p h t", h=GROUPS), ident_bf[:, :],
                   causal_bf[:, :].unsqueeze(1).to_broadcast([P, GROUPS, T]), start=True, stop=False,
                   skip_group_check=True)
                for j in range(GROUPS):
                    last = mm(psum[:, bank, j * T:(j + 1) * T], qf_stack[0:MAX_ROW, b.slot(), GROUPS * n + j, :],
                              kf_stack[0:MAX_ROW, b.slot(4), :], start=False, stop=(j == GROUPS - 1),
                              skip_group_check=True)
                last.then_inc(S["f_scores_max"], 1)

            def f_turn_max(b, half):
                pe.wait_ge(S["f_max_split"], b.times(2, half + 1))
                nc.tensor.transpose(psum[0:LEVELS * HALF, BANK_B, 0:P // 2].bitcast(BF16), maxf_levels[:, :],
                                    ident_bf[:, :]).then_inc(S["f_maxT_mm"], 1)

            def f_exp_scores(b, n):
                if n % 2 == 0:
                    pe.wait_ge(f_max_in[n // 2][b.slot()], b.uses(LEVELS * DMA, LEVELS * DMA))
                reached(pe, S["f_exp_done"], b, 4, n - 1)
                mm(psum[:, bank_exp[n % 2], :], kf_stack[:, b.slot(4), :],
                   qf_stack[:, b.slot(), GROUPS * n:GROUPS * (n + 1), :], start=True, stop=True)\
                    .then_inc(S["f_scores_exp"], 1)

            def f_value_product(b):
                pe.wait_ge(S["f_masked"], b.times(4, 4))
                pe.wait_ge(S["f_v_ready"], b.times(1, 1))
                reached(pe, S["f_pv_copied"], b, 1)
                for n in range(GROUPS):
                    last = mm(psum[32 * n:32 * (n + 1), BANK_PV, :], vf_cols[:, b.slot(V_RING), :],
                              probs_f[:, b.slot(), n * BANK:(n + 1) * BANK], start=True, stop=True)
                last.then_inc(S["f_pv_done"], 1)

            def f_turn_outputs(b):
                pe.wait_ge(S["f_pv_copied"], b.times(1, 1))
                for j in range(GROUPS):
                    last = nc.tensor.transpose(psum[:, BANK_C, j * P:(j + 1) * P], pvf_out[:, j * T:(j + 1) * T],
                                               ident[:, :])
                last.then_inc(S["f_outT_mm"], 1)

            def causal_step(s):
                before, nxt, nxt2, new = s + -1, s + 1, s + 2, s + 3
                for n in range(4):
                    if live(nxt):
                        f_max_scores(nxt, n)
                    if live(s):
                        f_exp_scores(s, n)
                    if n == 0:
                        if live(s):
                            pe.wait_ge(S["f_maxT_copied"], s.times(2, 1))
                            if live(nxt):
                                pe.wait_ge(S["f_kT"], nxt.times(1, 1))
                            f_turn_max(s, 1)
                        if live(before):
                            f_value_product(before)
                    if n == 1 and live(new):
                        if live(s):
                            pe.wait_ge(S["f_maxT_copied"], s.times(2, 2))
                        elif live(nxt):
                            pe.wait_ge(S["f_kT"], nxt.times(1, 1))
                        f_turn_x(new)
                    if n == 2 and live(before):
                        if live(nxt2):
                            pe.wait_ge(S["f_q_copied"], nxt2.times(1, 1))
                        reached(pe, S["f_y_ready"], before, 1)
                        f_turn_outputs(before)
                    if n == 3:
                        if live(nxt):
                            if live(new):
                                pe.wait_ge(S["f_xnT"], new.times(1, 1))
                            elif live(s):
                                pe.wait_ge(S["f_maxT_copied"], s.times(2, 2))
                            f_turn_max(nxt, 0)
                        if live(nxt2):
                            if live(nxt):
                                pe.wait_ge(S["f_maxT_copied"], nxt.times(2, 1))
                            if live(new):
                                pe.wait_ge(S["f_xnT"], new.times(1, 1))
                            f_turn_k(nxt2)
                        if live(new):
                            if live(before):
                                pe.wait_ge(S["f_y_ready"], before.times(1, 1))
                            f_project_gq(new)
                            f_project_kv(new)

            schedule(pe, causal_step)

        @block.scalar
        def _(act):
            def copy(dst, src, bias=0.0, scale=1.0, function=ACT.Copy):
                return nc.scalar.activation(dst, src, function, bias=bias, scale=scale)

            act.wait_ge(S["small_in"], 5 * DMA)
            nc.scalar.activation(gates[:, :], gates_in[:, :], ACT.Tanh).then_inc(S["tanh_done"], 1)
            for n, scale in enumerate((XATTN_SCALE, 1.0)):
                copy(bias_perm[:, n, :].rearrange("a (d h) -> a d h", h=H),
                     bias_rows[:, n, :].rearrange("a (h d) -> a d h", d=DX), scale=scale).then_inc(S["bias_ordered"], 1)
            act.wait_ge(S["bias_mm"], 1)
            copy(bias_col[:, 0:1], psum[:, BANK_B, 0:1]).then_inc(S["bias_copied"], 1)
            copy(bias_col[:, 1:2], psum[:, BANK_B, 1:2]).then_inc(S["bias_copied"], 1)
            act.wait_ge(S["maskT_mm"], 1)
            copy(mask_col[:, :], psum[:, BANK_C, 0:B * PT]).then_inc(S["maskcol_ready"], 1)

            def cross_step(s):
                before, nxt, new = s + -1, s + 1, s + 3

                def copy_max(b, half):
                    n = LEVELS * HALF * PT
                    act.wait_ge(S["maxT_mm"], b.times(2, half + 1))
                    if b.c >= 1:
                        last = b + -1
                        act.wait_ge(max_in[half][last.slot()], last.uses(LEVELS * DMA, LEVELS * DMA))
                    copy(max_rows[:, half, :], psum[0:n, BANK_B, 0:P // 2].bitcast(BF16)).then_inc(S["maxT_copied"], 1)

                if s.k is None and s.c == -1:
                    act.wait_ge(S["wf_transposed"], 1)
                    for c in range(PT):
                        copy(wfT[:, c, 0:C].rearrange("p (d h) -> p h d", h=H),
                             psum[:, bank_exp[0], c * C:(c + 1) * C].rearrange("p (h d) -> p h d", h=H),
                             scale=FFN_SCALE).then_inc(S["wf_copied"], 1)
                    for n, bank in enumerate((bank_exp[1], BANK_PV)):
                        copy(wfT[:, :, (n + 1) * C:(n + 2) * C],
                             psum[:, bank, :].rearrange("p (c o) -> p c o", c=PT)).then_inc(S["wf_copied"], 1)
                    copy(wgT[:, :, :], psum[:, BANK_C, 0:PT * H].rearrange("p (c h) -> p c h", c=PT))\
                        .then_inc(S["wf_copied"], 1)
                for h in range(H):
                    quad, j = divmod(h, GROUPS)
                    if live(s):
                        act.wait_ge(S["scores_exp"], s.times(H, h + 1))
                        if j == 0:
                            reached(act, S["pv_done"], s, 4, quad - 3)
                        nc.scalar.activation(probs[:, quad, j, :], psum[:, bank_exp[h % 2], :], ACT.Exp)\
                            .then_inc(S["exp_done"], 1)
                    if h == 2 and live(s):
                        copy_max(s, 1)
                    if h == 4 and live(before):
                        act.wait_ge(S["pv_done"], before.times(4, 4))
                        reached(act, S["outT_mm"], before, 1)
                        copy(pv_out[:, :], psum[:, BANK_PV, :]).then_inc(S["pv_copied"], 1)
                    if h == 5 and live(new):
                        act.wait_ge(S["qk_mm"], new.times(1, 1))
                        reached(act, S["qk_masked"], new, 1)
                        if s.k is None and s.c == -3:
                            act.wait_ge(S["bias_copied"], 2)
                        for n in range(2):
                            last = copy(qk_raw[:, n, :], psum[:, BANK_A, n * C:(n + 1) * C], bias=bias_col[:, n:n + 1],
                                        function=ACT.Identity)
                        last.then_inc(S["qk_copied"], 1)
                    if h == 8 and live(new):
                        act.wait_ge(S["qk_masked"], new.times(1, 1))
                        if new.c >= 1:
                            last = new + -1
                            act.wait_ge(levels_out[last.slot()], last.uses(2 * DMA, 2 * DMA))
                        copy(qk_levels[:, :, 0, :], qk_f[:, :, :]).then_inc(S["qk_high"], 1)
                    if h == 10 and live(new):
                        act.wait_ge(S["qk_resid"], new.times(1, 1))
                        copy(qk_levels[:, :, 1, :], qk_rest[:, :, :]).then_inc(S["qk_mid"], 1)
                    if h == 12 and live(nxt):
                        copy_max(nxt, 0)

            schedule(act, cross_step)

            def causal_step(s):
                before, nxt, nxt2, new = s + -1, s + 1, s + 2, s + 3

                def copy_max(b, half):
                    act.wait_ge(S["f_maxT_mm"], b.times(2, half + 1))
                    if b.c >= 1:
                        last = b + -1
                        act.wait_ge(f_max_in[half][last.slot()], last.uses(LEVELS * DMA, LEVELS * DMA))
                    copy(maxf_rows[:, half, :], psum[0:LEVELS * HALF, BANK_B, 0:P // 2].bitcast(BF16))\
                        .then_inc(S["f_maxT_copied"], 1)

                for n in range(4):
                    if live(s):
                        act.wait_ge(S["f_scores_exp"], s.times(4, n + 1))
                        if n == 0:
                            reached(act, S["f_pv_done"], s, 1, -1)
                        nc.scalar.activation(probs_f[:, s.slot(), n * BANK:(n + 1) * BANK], psum[:, bank_exp[n % 2], :],
                                             ACT.Exp).then_inc(S["f_exp_done"], 1)
                    if n == 0:
                        if live(s):
                            copy_max(s, 1)
                        if live(nxt2):
                            act.wait_ge(S["f_gq_mm"], nxt2.times(1, 1))
                            reached(act, S["f_q_low"], nxt2, 1)
                            if nxt2.c >= 1:
                                last = nxt2 + -1
                                act.wait_ge(f_levels_out[last.slot()], last.uses(PT * DMA, PT * DMA))
                            reached(act, S["f_selected"], nxt2, 1)
                            copy(logit[:, :], psum[:, BANK_C, PT * T:PT * T + H])
                            copy(qf_f[:, :], psum[:, BANK_C, 0:PT * T]).then_inc(S["f_q_copied"], 1)
                            act.wait_ge(S["f_q_copied"], nxt2.times(1, 1))
                            copy(qf_lev[:, 0, :], qf_f[:, :]).then_inc(S["f_q_high"], 1)
                            act.wait_ge(S["f_logit"], nxt2.times(1, 1))
                            reached(act, S["f_v_ready"], nxt2, 1)
                            nc.scalar.activation(gate_e[:, :], logit[:, :], ACT.Exp, bias=top_neg[:, 0:1],
                                                 accum_out=gate_sum[:, 0:1]).then_inc(S["f_gate_e"], 1)
                            act.wait_ge(S["f_q_resid"], nxt2.times(1, 1))
                            copy(qf_lev[:, 1, :], qf_rest[:, :]).then_inc(S["f_q_mid"], 1)
                    if n == 1:
                        if live(new):
                            act.wait_ge(S["f_xnT_mm"], new.times(1, 1))
                            reached(act, S["f_kv_mm"], new, 1)
                            copy(xnT[:, :, :], psum[:, BANK_B, 0:PT * T].rearrange("p (c t) -> p c t", c=PT))\
                                .then_inc(S["f_xnT"], 1)
                        if live(before):
                            act.wait_ge(S["f_pv_done"], before.times(1, 1))
                            reached(act, S["f_outT_mm"], before, 1)
                            copy(pvf_out[:, :], psum[:, BANK_PV, :]).then_inc(S["f_pv_copied"], 1)
                    if n == 3:
                        if live(nxt):
                            copy_max(nxt, 0)
                        if live(nxt2):
                            act.wait_ge(S["f_kT_mm"], nxt2.times(1, 1))
                            copy(kf_stack[:, nxt2.slot(4), :], psum[0:ROWS, BANK_B, 0:T // 2].bitcast(BF16))\
                                .then_inc(S["f_kT"], 1)

            schedule(act, causal_step)

        @block.vector
        def _(dve):
            chain = Chain(dve, S["dve_chain"])
            v = nc.vector

            for i in range(2):
                v.memset(k_stack[MAX_ROW:ROWS, i, :, :], 1.0).then_inc(S["memset_done"], 1)
                for st in (q_stack, k_stack):
                    v.memset(st[0:MAX_ROW, i, :, :].bitcast(F32), 0.0).then_inc(S["memset_done"], 1)
                if i == 0:
                    dve.wait_ge(S["w_transposed"], 1)
                    v.tensor_scalar(wT[:, 0, :].rearrange("p (d h) -> p h d", h=H),
                                    psum[:, BANK_A, 0:P].rearrange("p (h d) -> p h d", h=H),
                                    XATTN_SCALE, None, ALU.mult).then_inc(S["w_copied"], 1)
                    v.tensor_copy(wT[:, 1, :].rearrange("p (d h) -> p h d", h=H),
                                  psum[:, BANK_A, P:2 * P].rearrange("p (h d) -> p h d", h=H)).then_inc(S["w_copied"], 1)
                    v.tensor_copy(wT[:, 2, :], psum[:, BANK_A, 2 * P:3 * P]).then_inc(S["w_copied"], 1)
                    dve.wait_ge(S["mask_in"], 2 * DMA)
                    v.tensor_copy(aug_f[:, 0, :], mask_b[:, :])
                    chain(v.tensor_scalar(aug_f[:, 1, :], mask_b[:, :], 1.0, NEG, ALU.subtract, ALU.mult))
                    chain(v.tensor_copy(aug_levels[:, :, 0, :], aug_f[:, :, :]))
                    chain(v.tensor_tensor(aug_r[:, :, :], aug_f[:, :, :], aug_levels[:, :, 0, :], ALU.subtract))
                    chain(v.tensor_copy(aug_levels[:, :, 1, :], aug_r[:, :, :]))
                    v.tensor_tensor(aug_levels[:, :, 2, :], aug_r[:, :, :], aug_levels[:, :, 1, :], ALU.subtract)\
                        .then_inc(S["aug_ready"], 1)
            dve.wait_ge(S["maskcol_ready"], 1)
            dve.wait_ge(S["tanh_done"], 1)
            chain(v.tensor_scalar(mask_gate[:, :], mask_col[:, :], gates[:, 0:1], None, ALU.mult))
            dve.wait_ge(S["small_in"], 5 * DMA)
            dve.wait_ge(S["pool_chain"], 10)

            def split_max(b, half, neg, levels, rest, taken, taken_per_batch, turned, signal):
                n = neg.shape[1]
                dve.wait_ge(taken, b.times(taken_per_batch, taken_per_batch // 2 * (half + 1)))
                reached(dve, turned, b, 2, half)
                chain(v.tensor_copy(levels[:, 0:n], neg))
                chain(v.tensor_tensor(rest, neg, levels[:, 0:n], ALU.subtract))
                chain(v.tensor_copy(levels[:, n:2 * n], rest))
                v.tensor_tensor(levels[:, 2 * n:3 * n], rest, levels[:, n:2 * n], ALU.subtract).then_inc(signal, 1)

            def cross_split(b, half):
                split_max(b, half, neg_max[:, half * HALF:(half + 1) * HALF, :].rearrange("p h t -> p (h t)"),
                          max_levels, max_rest[:, :], S["max_taken"], H, S["maxT_mm"], S["max_split"])

            def moments(b, st, mv, r, signal):
                v.bn_stats(st[:, :], xs[:, b.index, :]).then_inc(S["dve_chain"], 1)
                chain.n += 1
                wait_apart(dve, (S["tanh_done"], 1), (S["dve_chain"], chain.base + chain.n))
                chain(v.bn_aggr(mv[:, :], st[:, :]))
                v.tensor_scalar(r[:, 0:1], mv[:, 1:2], EPS, None, ALU.add).then_inc(signal, 1)

            def normalise(b, dst, mv, r, signal):
                v.tensor_scalar(dst[:, :], xs[:, b.index, :], mv[:, 0:1], r[:, 1:2], ALU.subtract, ALU.mult)\
                    .then_inc(signal, 1)

            def normalise_outputs(b):
                dve.wait_ge(S["outT_mm"], b.times(1, 1))
                rows = psum[:, BANK_A, :].rearrange("p (g j x) -> p g j x", g=2 * PT, j=GROUPS)
                chain(v.reciprocal(recip[:, :].rearrange("p (g j s) -> p g j s", g=2 * PT, j=GROUPS),
                                   rows[:, :, :, 2 * DX:2 * DX + 2]))
                chain(v.tensor_tensor(recip_g[:, :].rearrange("p (t n) -> p t n", t=PT),
                                      recip[:, :].rearrange("p (t n) -> p t n", t=PT),
                                      mask_gate[:, bass.ds(b.times(PT), PT)].unsqueeze(2).to_broadcast([P, PT, 2 * 8]),
                                      ALU.mult))
                reached(dve, S["attnT_mm"], b, 1)
                dst = attn_t[:, :, :].rearrange("p t (r s j d) -> p (t r) s j d", r=2, s=2, j=GROUPS)
                scale = recip_g[:, :].rearrange("p (g j s) -> p g j s", g=2 * PT, j=GROUPS)
                for slot in range(2):
                    last = v.tensor_tensor(dst[:, :, slot, :, :], rows[:, :, :, slot * DX:(slot + 1) * DX],
                                           scale[:, :, :, slot].unsqueeze(3).to_broadcast([P, 2 * PT, GROUPS, DX]),
                                           ALU.mult)
                last.then_inc(S["attn_normed"], 1)

            def cross_step(s):
                before, nxt, new = s + -1, s + 1, s + 3
                if live(s):
                    cross_split(s, 1)
                for h in range(H):
                    if live(nxt):
                        dve.wait_ge(S["scores_max"], nxt.times(H, h + 1))
                        v.tensor_reduce(out=neg_max[:, h, :], in_=psum[:, bank_max[h % 2], :]
                                        .rearrange("p (t c) -> p t c", t=PT), op=ALU.max, axis=AX.X, negate=True)\
                            .then_inc(S["max_taken"], 1)
                    if h == 0 and live(new):
                        if s.k is None and s.c == -3:
                            dve.wait_ge(S["x_first"], DMA)
                        if s.k is None and s.c == 0:
                            dve.wait_ge(S["x_rest"], DMA)
                        moments(new, stats, meanvar, rstd, S["norm_stats"])
                    if h == 1 and live(new):
                        dve.wait_ge(S["rstd_ready"], new.times(1, 1))
                        reached(dve, S["qk_mm"], new, 1)
                        normalise(new, xn, meanvar, rstd, S["xn_ready"])
                    if h == 8 and live(nxt):
                        cross_split(nxt, 0)
                    if h == 9 and live(new):
                        dve.wait_ge(S["v_mm"], new.times(1, 1))
                        reached(dve, S["v_ready"], new, 1)
                        v.tensor_tensor(v_sum[:, :, :], psum[:, BANK_B, 0:PT * P].rearrange("p (t o) -> p t o", t=PT),
                                        bv_all[:, :].unsqueeze(1).to_broadcast([P, PT, P]), ALU.add)\
                            .then_inc(S["v_added"], 1)
                    if h == 11 and live(before):
                        normalise_outputs(before)
                    if h == 15 and live(before):
                        dve.wait_ge(S["attnT_mm"], before.times(1, 1))
                        v.tensor_tensor(xs[:, before.index, :], psum[:, BANK_B, 0:C], xs[:, before.index, :], ALU.add)\
                            .then_inc(S["x_updated"], 1)

            schedule(dve, cross_step, chain, 10)

            dve.wait_ge(S["const_ready"], 3)

            def causal_split(b, half):
                split_max(b, half, neg_max_f[:, half * HALF:(half + 1) * HALF], maxf_levels, maxf_rest[:, 0:HALF],
                          S["f_max_taken"], 4, S["f_maxT_mm"], S["f_max_split"])

            def choose_head(b):
                dve.wait_ge(S["f_q_copied"], b.times(1, 1))
                v.tensor_reduce(out=top_neg[:, 0:1], in_=logit[:, :], op=ALU.max, axis=AX.X, negate=True)\
                    .then_inc(S["f_logit"], 1)
                dve.wait_ge(S["f_logit"], b.times(1, 1))
                chain(v.tensor_scalar(rank[:, :], logit[:, :], top_neg[:, 0:1], 0.0, ALU.add, ALU.is_ge))
                chain(v.tensor_tensor(rank[:, :], rank[:, :], first_head[:, :], ALU.mult))
                chain(v.tensor_reduce(out=rank_top[:, :], in_=rank[:, :], op=ALU.max, axis=AX.X))
                chain(v.tensor_scalar(chosen[:, :], rank[:, :], rank_top[:, 0:1], None, ALU.is_ge))

            def select_head(b):
                dve.wait_ge(S["f_kv_mm"], b.times(1, 1))
                v.tensor_tensor(kv_sel[:, :, :, :], psum[:, BANK_A, :].rearrange("p (k h d) -> p k h d", k=2, h=H),
                                chosen[:, :].unsqueeze(1).unsqueeze(3).to_broadcast([P, 2, H, DF]), ALU.mult)\
                    .then_inc(S["f_selected"], 1)
                dve.wait_ge(S["f_selected"], b.times(1, 1))
                chain(v.tensor_reduce(out=kv_one[:, :, :], in_=kv_sel[:, :, :, :].rearrange("p k h d -> p k d h"),
                                      op=ALU.add, axis=AX.X))

            def lay_out_k(b):
                reached(dve, S["f_kT_mm"], b, 1)
                k_rows = kf_rows[:, 0:MAX_ROW].rearrange("p (g d) -> p g d", d=DF)
                kk = kv_one[:, 0, :].unsqueeze(1)
                chain(v.tensor_copy(k_rows[:, 0:3, :], kk.to_broadcast([P, 3, DF])))
                chain(v.tensor_tensor(kf_rest[:, :, :], kk.to_broadcast([P, 2, DF]), k_rows[:, 0:2, :], ALU.subtract))
                chain(v.tensor_copy(k_rows[:, 3:5, :], kf_rest[:, :, :]))
                v.tensor_tensor(k_rows[:, 5, :], kf_rest[:, 0, :], k_rows[:, 3, :], ALU.subtract).then_inc(S["f_kT_in"], 1)
                dve.wait_ge(S["f_gate_e"], b.times(1, 1))
                chain(v.reciprocal(gate_sum[:, 1:2], gate_sum[:, 0:1]))
                reached(dve, S["f_pv_done"], b, 1, -3)
                v.tensor_scalar(vf_cols[:, b.slot(V_RING), 0:DF], kv_one[:, 1, :], gate_sum[:, 1:2], None, ALU.mult)\
                    .then_inc(S["f_v_ready"], 1)

            def finish(b):
                dve.wait_ge(S["f_outT_mm"], b.times(1, 1))
                rows = psum[:, BANK_C, :].rearrange("p (j g x) -> p j g x", j=GROUPS, g=GROUPS)
                chain(v.reciprocal(recip_f[:, :].rearrange("p (j g) -> p j g", j=GROUPS), rows[:, :, :, DF]))
                chain(v.tensor_scalar(recip_fg[:, :], recip_f[:, :], gates[:, 1:2], None, ALU.mult))
                v.tensor_tensor(y_f[:, :].rearrange("p (g j d) -> p j g d", g=GROUPS, j=GROUPS), rows[:, :, :, 0:DF],
                                recip_fg[:, :].rearrange("p (j g) -> p j g", j=GROUPS).unsqueeze(3)
                                .to_broadcast([P, GROUPS, GROUPS, DF]), ALU.mult).then_inc(S["f_y_ready"], 1)
                dve.wait_ge(S["f_y_ready"], b.times(1, 1))
                if b.k is not None or b.c >= 2:
                    dve.wait_ge(out_written[b.slot()], b.uses(DMA))
                v.tensor_tensor(out_sb[:, b.slot(), :], y_f[:, :], xs[:, b.index, :], ALU.add)\
                    .then_inc(S["f_out_ready"], 1)

            def causal_step(s):
                before, nxt, nxt2, new = s + -1, s + 1, s + 2, s + 3
                if live(new):
                    if s.k is None and s.c == -3:
                        dve.wait_ge(S["x_updated"], B)
                    moments(new, stats_f, meanvar_f, rstd_f, S["f_stats"])
                if live(s):
                    causal_split(s, 1)
                for n in range(4):
                    if live(nxt):
                        dve.wait_ge(S["f_scores_max"], nxt.times(4, n + 1))
                        v.tensor_reduce(out=neg_max_f[:, n * GROUPS:(n + 1) * GROUPS], in_=psum[:, bank_max[n % 2], :]
                                        .rearrange("p (h t) -> p h t", h=GROUPS), op=ALU.max, axis=AX.X, negate=True)\
                            .then_inc(S["f_max_taken"], 1)
                    if n == 0:
                        if live(new):
                            dve.wait_ge(S["f_rstd"], new.times(1, 1))
                            reached(dve, S["f_xnT_mm"], new, 1)
                            normalise(new, xn_f, meanvar_f, rstd_f, S["f_xn"])
                        if live(nxt2):
                            choose_head(nxt2)
                    if n == 1 and live(nxt2):
                        select_head(nxt2)
                    if n == 2:
                        if live(nxt):
                            causal_split(nxt, 0)
                        if live(nxt2):
                            lay_out_k(nxt2)
                        if live(before):
                            finish(before)

            schedule(dve, causal_step, chain, 19)


_INS = ['x', 'ctx_2048', 'mask_Bx1x2048_fk1', 'g_xattn', 'g_ffn', 'L0_xattn_Wq', 'L0_xattn_bq', 'L0_xattn_Wk',
        'L0_xattn_bk', 'L0_xattn_Wv', 'L0_xattn_bv', 'L0_ffn_W_gate', 'L0_ffn_W_qkv']


def kernel(**inputs):
    import numpy as _np
    import concourse.bacc as _bacc
    from concourse import mybir as _mybir
    from concourse.bass_utils import run_bass_kernel_spmd as _run

    nc = _bacc.Bacc("TRN2", target_bir_lowering=False, num_devices=1)
    arrays, args = {}, []
    for name in _INS:
        a = _np.ascontiguousarray(inputs[name])
        arrays[f"in_{name}"] = a
        args.append(nc.dram_tensor(f"in_{name}", a.shape, _mybir.dt.from_np(a.dtype), kind="ExternalInput").ap())
    x = inputs["x"]
    out = nc.dram_tensor("out", x.shape, _mybir.dt.float32, kind="ExternalOutput").ap()
    flamingo_kernel(nc, *args, out)
    r = _run(nc, [arrays], core_ids=[0])
    return r.results[0]["out"]
```

```python
from contextlib import ExitStack

import concourse.bass as bass
from concourse import mybir

F32 = mybir.dt.float32
BF16 = mybir.dt.bfloat16
ALU = mybir.AluOpType
ACT = mybir.ActivationFunctionType
AX = mybir.AxisListType

P = 128
LEVELS = 3
BANK = 512
EPS = 1e-5
NEG = 1000000.0

PAIRS = [(0, 0), (1, 0), (2, 0), (0, 1), (1, 1), (0, 2)]
Q_RUNS = [(0, 0, 3), (3, 0, 2), (5, 0, 1)]
K_RUNS = [(0, 0, 3), (3, 1, 2), (5, 2, 1)]
MAX_ROW = 96
ROWS = MAX_ROW + LEVELS
RING = 4
LAG = 6
CAUSAL_LAG = 2
DMA = 16


class Batch:

    def __init__(self, c, k=None, m=0):
        self.c, self.k, self.m = c, k, m

    def __add__(self, n):
        return Batch(self.c + n, self.k, self.m)

    def times(self, f, extra=0):
        return f * self.c + extra if self.k is None else self.k * (f * self.m) + (f * self.c + extra)

    def uses(self, f, extra=0, ring=2):
        n = f * (self.c // ring) + extra
        assert n > 0
        return n if self.k is None else self.k * (f * self.m // ring) + n

    @property
    def index(self):
        return self.times(1)

    @property
    def least(self):
        return self.c

    def slot(self, ring=2):
        return self.c % ring


def reached(eng, semaphore, b, per_batch, extra=0):
    first = per_batch * b.c + extra
    if b.k is None:
        if first > 0:
            eng.wait_ge(semaphore, first)
    else:
        assert first > 0
        eng.wait_ge(semaphore, b.times(per_batch, extra))


def wait_apart(eng, held, *waits):
    values = [(semaphore, v if isinstance(v, int) else eng.to_reg(v)) for semaphore, v in waits]
    eng.wait_ge(*held)
    for semaphore, v in values:
        if not isinstance(v, int) or v > 0:
            eng.wait_ge(semaphore, v)


class Chain:

    def __init__(self, eng, sem):
        self.eng, self.sem, self.base, self.n = eng, sem, 0, 0

    def __call__(self, instruction):
        instruction.then_inc(self.sem, 1)
        self.n += 1
        self.eng.wait_ge(self.sem, self.base + self.n)

    def enter(self, k, per_turn):
        self.start = self.base + self.n
        self.base, self.n, self.per_turn = k * per_turn + self.start, 0, per_turn

    def leave(self, turns):
        assert self.n == self.per_turn, (self.n, self.per_turn)
        self.base, self.n = self.start + turns * self.per_turn, 0


def flamingo_kernel(nc, x, ctx_in, mask, g_xattn, g_ffn, Wq, bq, Wk, bk, Wv, bv, W_gate, W_qkv, out):
    B, T, C = x.shape
    H = W_gate.shape[0]
    DX = T // H
    DF = C // H
    PT = C // P
    GROUPS = 4
    CHX = DX + 1
    PAIR_ROWS_X = len(PAIRS) * CHX
    assert T == P and C == PT * P and PAIR_ROWS_X <= MAX_ROW and len(PAIRS) * DF == MAX_ROW
    assert P // GROUPS >= 2 * DX + 2 and H == GROUPS * GROUPS
    XATTN_SCALE = float(DX) ** -0.5
    FFN_SCALE = float(DF) ** -0.5

    levels = nc.dram_tensor("levels", (B, 2, LEVELS, CHX, H, C), BF16).ap()
    qf_levels = nc.dram_tensor("qf_levels", (B, LEVELS, DF, H, T), BF16).ap()

    with ExitStack() as stack:
        def sb(name, shape, dt=F32):
            return stack.enter_context(nc.sbuf_tensor(name, shape, dt))

        def sem(name):
            return stack.enter_context(nc.semaphore(name))

        psum = stack.enter_context(nc.psum_tensor("psum", [P, 8, BANK], F32))
        bank_max = [0, 1]
        bank_exp = [2, 3]
        BANK_PV, BANK_A, BANK_B, BANK_C = 4, 5, 6, 7

        ident = sb("ident", [P, P])
        ident_bf = sb("ident_bf", [P, P], BF16)
        causal_bf = sb("causal_bf", [P, P], BF16)
        ones_row = sb("ones_row", [1, P])
        half_power = sb("half_power", [P, 1])
        first_head = sb("first_head", [P, H])
        w_rows = sb("w_rows", [P, 3, P])
        wqkv_rows = sb("wqkv_rows", [P, 3 * C // P, C])
        wgate_rows = sb("wgate_rows", [H, C])
        wT = sb("wT", [P, 3, P])
        bias_rows = sb("bias_rows", [1, 2, P])
        bias_perm = sb("bias_perm", [1, 2, P])
        bias_col = sb("bias_col", [P, 2])
        bv_all = sb("bv_all", [P, P])
        gates_in = sb("gates_in", [P, 2])
        gates = sb("gates", [P, 2])
        mask_rows = sb("mask_rows", [B * PT, P])
        mask_col = sb("mask_col", [P, B * PT])
        mask_gate = sb("mask_gate", [P, B * PT])
        mask_b = sb("mask_b", [B, C])
        aug_f = sb("aug_f", [B, 2, C])
        aug_r = sb("aug_r", [B, 2, C])
        aug_levels = sb("aug_levels", [B, 2, LEVELS, C], BF16)
        wfT = sb("wfT", [P, PT, 3 * C])
        wgT = sb("wgT", [P, PT, H])

        xs = sb("xs", [P, B, C])
        ctx = sb("ctx", [P, 2, C])
        mask_all = sb("mask_all", [P, 2, C])
        stats = sb("stats", [P, 6])
        meanvar = sb("meanvar", [P, 2])
        rstd = sb("rstd", [P, 2])
        xn = sb("xn", [P, C])
        qk_raw = sb("qk_raw", [P, 2, C])
        qk_f = sb("qk_f", [P, 2, C])
        qk_rest = sb("qk_rest", [P, 2, C])
        qk_levels = sb("qk_levels", [P, 2, LEVELS, C], BF16)
        v_sum = sb("v_sum", [P, PT, P])
        v_cols = sb("v_cols", [P, RING, PT, H, 32])
        q_stack = sb("q_stack", [ROWS, RING, H, C], BF16)
        k_stack = sb("k_stack", [ROWS, RING, H, C], BF16)
        zero_rows = sb("zero_rows", [MAX_ROW - PAIR_ROWS_X, H, C], BF16)
        one_rows = sb("one_rows", [LEVELS, H, C], BF16)
        neg_max = sb("neg_max", [P, H * PT])
        max_rest = sb("max_rest", [P, H * PT])
        max_levels = sb("max_levels", [P, LEVELS * H * PT], BF16)
        max_rows = sb("max_rows", [LEVELS * H * PT, P], BF16)
        probs = sb("probs", [P, 2, GROUPS, PT * C])
        pv_out = sb("pv_out", [P, 2 * C])
        recip = sb("recip", [P, 32])
        recip_g = sb("recip_g", [P, 32])
        attn_t = sb("attn_t", [P, PT, P])

        stats_f = sb("stats_f", [P, 6])
        meanvar_f = sb("meanvar_f", [P, 2])
        rstd_f = sb("rstd_f", [P, 2])
        xn_f = sb("xn_f", [P, C])
        xnT = sb("xnT", [P, PT, T])
        qf_f = sb("qf_f", [P, PT * T])
        qf_rest = sb("qf_rest", [P, PT * T])
        qf_lev = sb("qf_lev", [P, LEVELS, PT * T], BF16)
        logit = sb("logit", [P, H])
        top_neg = sb("top_neg", [P, 2])
        gate_e = sb("gate_e", [P, H])
        gate_sum = sb("gate_sum", [P, 2])
        rank = sb("rank", [P, H])
        rank_top = sb("rank_top", [P, 1])
        chosen = sb("chosen", [P, H])
        kv_sel = sb("kv_sel", [P, 2, H, DF])
        kv_one = sb("kv_one", [P, 2, DF])
        kf_rest = sb("kf_rest", [P, 2, DF])
        kf_rows = sb("kf_rows", [P, ROWS], BF16)
        vf_cols = sb("vf_cols", [P, RING, P // GROUPS])
        kf_stack = sb("kf_stack", [ROWS, RING, T], BF16)
        neg_max_f = sb("neg_max_f", [P, H])
        maxf_rest = sb("maxf_rest", [P, H])
        maxf_levels = sb("maxf_levels", [P, LEVELS * H], BF16)
        maxf_rows = sb("maxf_rows", [LEVELS * H, P], BF16)
        probs_f = sb("probs_f", [P, 2, H * T])
        pvf_out = sb("pvf_out", [P, BANK])
        recip_f = sb("recip_f", [P, H])
        recip_fg = sb("recip_fg", [P, H])
        y_f = sb("y_f", [P, C])

        S = {}
        for name in (
            "weights_in small_in x_first x_rest mask_in qkv_in "
            "const_ready pool_chain dve_chain fill_ready filled causal_ready w_transposed w_copied wf_transposed wf_copied "
            "bias_ordered bias_mm bias_copied tanh_done aug_ready maskT_mm maskcol_ready aug_written vcols_ready "
            "norm_stats rstd_ready xn_ready qk_mm v_mm qk_copied v_added qk_masked qk_high qk_resid qk_mid qk_low v_ready "
            "scores_max max_taken max_split maxT_mm maxT_copied scores_exp exp_done pv_done pv_copied "
            "outT_mm attn_normed attnT_mm x_updated "
            "f_stats f_rstd f_xn f_xnT_mm f_xnT f_kv_mm f_gq_mm f_logit f_gate_e f_selected f_q_copied f_q_high f_q_resid f_q_mid "
            "f_q_low f_kT_in f_kT_mm f_kT f_v_ready f_scores_max f_max_taken f_max_split f_maxT_mm f_maxT_copied f_scores_exp "
            "f_exp_done f_masked f_pv_done f_pv_copied f_outT_mm f_y_ready f_out_ready"
        ).split():
            S[name] = sem(name)
        in_loaded = [sem(f"in_loaded{i}") for i in range(2)]
        levels_out = [sem(f"levels_out{i}") for i in range(2)]
        stack_in = [sem(f"stack_in{i}") for i in range(2)]
        max_in = [sem(f"max_in{i}") for i in range(2)]
        f_levels_out = [sem(f"f_levels_out{i}") for i in range(2)]
        f_stack_in = [sem(f"f_stack_in{i}") for i in range(2)]
        f_max_in = [sem(f"f_max_in{i}") for i in range(2)]
        out_written = sem("out_written")
        STACK_DMAS = len(Q_RUNS) + len(K_RUNS)

        def schedule(eng, cross_step, causal_step, chain=None, cross_per_step=0, causal_per_step=0):
            unroll = RING
            turns = (B - 4) // unroll
            assert turns * unroll == B - 4
            for step, per_step, joined in ((cross_step, cross_per_step, 0), (causal_step, causal_per_step, 3)):
                for s in range(-3 + joined, 1):
                    step(Batch(s))
                with eng.Fori(0, turns) as k:
                    if chain:
                        chain.enter(k, per_step * unroll)
                    for u in range(unroll):
                        step(Batch(1 + u, k, unroll))
                if chain:
                    chain.leave(turns)
                for s in range(B - 3, B + 1):
                    step(Batch(s))
                    if not joined and s - JOIN >= -3:
                        causal_step(Batch(s - JOIN))

        JOIN = B + 1

        def live(b):
            return b.k is not None or 0 <= b.c < B

        def lagged(s, n, lag, per_batch):
            return (s + -1, n - lag + per_batch) if n < lag else (s, n - lag)

        block = stack.enter_context(nc.Block())

        @block.sync
        def _(sp):
            for n, w in enumerate((Wq, Wk, Wv)):
                sp.dma_start(w_rows[:, n, :], w).then_inc(S["weights_in"], DMA)
            sp.dma_start(xs[:, 0:4, :], x[0:4].rearrange("b t c -> t b c")).then_inc(S["x_first"], DMA)
            for n, v in enumerate((bq, bk)):
                sp.dma_start(bias_rows[:, n, :], v.rearrange("(a n) -> a n", a=1)).then_inc(S["small_in"], DMA)
            sp.dma_start(bv_all[:, :], bv.rearrange("(a n) -> a n", a=1).to_broadcast([P, P])).then_inc(S["small_in"], DMA)
            for n, v in enumerate((g_xattn, g_ffn)):
                sp.dma_start(gates_in[:, n:n + 1], v.rearrange("(a n) -> a n", a=1).to_broadcast([P, 1]))\
                    .then_inc(S["small_in"], DMA)
            sp.dma_start(mask_rows[:, :], mask.rearrange("b a (t p) -> (b a t) p", p=P)).then_inc(S["mask_in"], DMA)
            sp.dma_start(mask_b[:, :], mask.rearrange("b a c -> (b a) c")).then_inc(S["mask_in"], DMA)

            sp.wait_ge(S["fill_ready"], 2)
            for i in range(RING):
                for st in (q_stack, k_stack):
                    sp.dma_start(st[PAIR_ROWS_X:MAX_ROW, i, :, :], zero_rows[:, :, :]).then_inc(S["filled"], DMA)
                sp.dma_start(k_stack[MAX_ROW:ROWS, i, :, :], one_rows[:, :, :]).then_inc(S["filled"], DMA)

            sp.wait_ge(S["aug_ready"], 1)
            for side in range(2):
                for l in range(LEVELS):
                    sp.dma_start(levels[:, side, l, DX], aug_levels[:, side, l].unsqueeze(1).to_broadcast([B, H, C]))\
                        .then_inc(S["aug_written"], DMA)

            loaded = (S["weights_in"], 3 * DMA)

            def load_inputs(b):
                if not live(b):
                    return
                wait_apart(sp, loaded, (S["v_mm"], b.times(1, -1)), (S["qk_masked"], b.times(1, -1)))
                sp.dma_start(ctx[:, b.slot(), :], ctx_in[b.index]).then_inc(in_loaded[b.slot()], DMA)
                sp.dma_start(mask_all[:, b.slot(), :], mask[b.index].to_broadcast([P, C]))\
                    .then_inc(in_loaded[b.slot()], DMA)

            def write_levels(b):
                if not live(b):
                    return
                wait_apart(sp, loaded, (S["qk_low"], b.times(1, 1)))
                sp.dma_start(levels[b.index][:, :, 0:DX].rearrange("s l d h c -> (d h) s l c"), qk_levels[:, :, :, :])\
                    .then_inc(levels_out[b.slot()], DMA)

            def load_stack(b):
                if not live(b):
                    return
                wait_apart(sp, loaded, (levels_out[b.slot()], b.uses(DMA, DMA)), (S["aug_written"], 2 * LEVELS * DMA))
                for pair, level, n in Q_RUNS:
                    sp.dma_start(q_stack[pair * CHX:(pair + n) * CHX, b.slot(RING), :, :],
                                 levels[b.index][0, level:level + n]).then_inc(stack_in[b.slot()], DMA)
                for pair, level, n in K_RUNS:
                    sp.dma_start(k_stack[pair * CHX:(pair + n) * CHX, b.slot(RING), :, :],
                                 levels[b.index][1, level:level + 1].to_broadcast([n, CHX, H, C]))\
                        .then_inc(stack_in[b.slot()], DMA)

            def load_max(b):
                if not live(b):
                    return
                wait_apart(sp, loaded, (S["maxT_copied"], b.times(1, 1)))
                sp.dma_start(q_stack[MAX_ROW:ROWS, b.slot(RING), :, :], max_rows[:, :]).then_inc(max_in[b.slot()], DMA)

            def cross_step(s):
                load_inputs(s + 3)
                if s.k is None and s.c == -3:
                    sp.dma_start(xs[:, 4:B, :], x[4:B].rearrange("b t c -> t b c")).then_inc(S["x_rest"], DMA)
                    sp.dma_start(wqkv_rows[:, :, :], W_qkv.rearrange("(n p) c -> p n c", p=P)).then_inc(S["qkv_in"], DMA)
                    sp.dma_start(wgate_rows[:, :], W_gate).then_inc(S["qkv_in"], DMA)
                load_max(s)
                load_stack(s + 2)
                write_levels(s + 3)

            def write_f_levels(b):
                if not live(b):
                    return
                wait_apart(sp, loaded, (S["f_q_low"], b.times(1, 1)))
                for t in range(PT):
                    n = DF // PT
                    sp.dma_start(qf_levels[b.index][:, t * n:(t + 1) * n].rearrange("l d h c -> (d h) l c"),
                                 qf_lev[:, :, t * T:(t + 1) * T]).then_inc(f_levels_out[b.slot()], DMA)

            def load_f_stack(b):
                if not live(b):
                    return
                wait_apart(sp, loaded, (f_levels_out[b.slot()], b.uses(PT * DMA, PT * DMA)))
                for pair, level, n in Q_RUNS:
                    sp.dma_start(q_stack[pair * DF:(pair + n) * DF, b.slot(RING), :, 0:T],
                                 qf_levels[b.index][level:level + n].rearrange("l d h c -> (l d) h c"))\
                        .then_inc(f_stack_in[b.slot()], DMA)

            def load_f_max(b):
                if not live(b):
                    return
                wait_apart(sp, loaded, (S["f_maxT_copied"], b.times(1, 1)))
                sp.dma_start(q_stack[MAX_ROW:ROWS, b.slot(RING), :, 0:T], maxf_rows[:, :])\
                    .then_inc(f_max_in[b.slot()], DMA)

            def store(b):
                if not live(b):
                    return
                wait_apart(sp, loaded, (S["f_out_ready"], b.times(1, 1)))
                sp.dma_start(out[b.index], xs[:, b.index, :]).then_inc(out_written, DMA)

            def causal_step(s):
                load_f_max(s)
                load_f_stack(s + 2)
                write_f_levels(s + 3)
                store(s + -1)

            schedule(sp, cross_step, causal_step)
            for i in range(2):
                sp.wait_ge(levels_out[i], B // 2 * DMA)
                sp.wait_ge(f_levels_out[i], B // 2 * PT * DMA)
            sp.wait_ge(S["aug_written"], 2 * LEVELS * DMA)
            sp.wait_ge(out_written, B * DMA)

        @block.gpsimd
        def _(pool):
            chain = Chain(pool, S["pool_chain"])
            nc.gpsimd.memset(one_rows[:, :, :], 1.0).then_inc(S["fill_ready"], 1)
            chain(nc.gpsimd.memset(ident[:, :], 0.0))
            chain(nc.gpsimd.affine_select(out=ident[:, :], in_=ident[:, :], compare_op=ALU.not_equal, fill=1.0, base=0,
                                          pattern=[[-1, P]], channel_multiplier=1))
            nc.gpsimd.tensor_copy(ident_bf[:, :], ident[:, :]).then_inc(S["const_ready"], 1)
            nc.gpsimd.memset(ones_row[:, :], 1.0).then_inc(S["const_ready"], 1)
            chain(nc.gpsimd.memset(half_power[:, :], -0.5))
            chain(nc.gpsimd.memset(v_cols[:, :, :, :, :], 0.0))
            for n in range(RING):
                for slot in range(2):
                    view = v_cols[:, n, :, :, :].rearrange("p t (r s j) x -> p (t r) s j x", s=2, j=GROUPS)
                    last = nc.gpsimd.memset(view[:, :, slot, :, 2 * DX + slot:2 * DX + slot + 1], 1.0)
                    last.then_inc(S["vcols_ready"], 1)
            pool.wait_ge(S["vcols_ready"], 2 * RING)
            chain(nc.gpsimd.memset(causal_bf[:, :], 0.0))
            chain(nc.gpsimd.affine_select(out=causal_bf[:, :], in_=causal_bf[:, :], compare_op=ALU.is_ge, fill=-1e30,
                                          base=0, pattern=[[-1, P]], channel_multiplier=1))
            chain(nc.gpsimd.memset(vf_cols[:, :, :], 0.0))
            chain(nc.gpsimd.memset(vf_cols[:, :, DF:DF + 1], 1.0))
            for h in range(H):
                nc.gpsimd.memset(first_head[:, h:h + 1], float(H - h))
            nc.gpsimd.memset(kf_rows[:, :], 1.0).then_inc(S["causal_ready"], 1)

            def inverse_std(r, ready, signal, b):
                pool.wait_ge(ready, b.times(1, 1))
                nc.gpsimd.tensor_tensor(r[:, 1:2], r[:, 0:1], half_power[:, :], ALU.pow).then_inc(signal, 1)

            def cross_step(s):
                bp = s + 3
                if live(bp):
                    inverse_std(rstd, S["norm_stats"], S["rstd_ready"], bp)
                    pool.wait_ge(S["qk_copied"], bp.times(1, 1))
                    pool.wait_ge(in_loaded[bp.slot()], bp.uses(2 * DMA, 2 * DMA))
                    nc.gpsimd.tensor_tensor(qk_f[:, :, :], qk_raw[:, :, :],
                                            mask_all[:, bp.slot(), :].unsqueeze(1).to_broadcast([P, 2, C]),
                                            ALU.mult).then_inc(S["qk_masked"], 1)
                    pool.wait_ge(S["qk_high"], bp.times(1, 1))
                    nc.gpsimd.tensor_tensor(qk_rest[:, :, :], qk_f[:, :, :], qk_levels[:, :, 0, :], ALU.subtract)\
                        .then_inc(S["qk_resid"], 1)
                    pool.wait_ge(S["v_added"], bp.times(1, 1))
                    if bp.k is None and bp.c == 0:
                        pool.wait_ge(S["maskcol_ready"], 1)
                    reached(pool, S["pv_done"], bp, 4, -12)
                    for t in range(PT):
                        for slot in range(2):
                            dst = v_cols[:, bp.slot(RING), t, :, :].rearrange("p (r s j) x -> p r s j x", s=2, j=GROUPS)
                            src = v_sum[:, t, :].rearrange("p (r s j d) -> p r s j d", s=2, j=GROUPS, d=DX)
                            col = mask_col[:, bass.ds(bp.times(PT, t), 1)]
                            last = nc.gpsimd.tensor_tensor(
                                dst[:, :, slot, :, slot * DX:(slot + 1) * DX], src[:, :, slot, :, :],
                                col.unsqueeze(2).unsqueeze(3).to_broadcast([P, 2, GROUPS, DX]), ALU.mult)
                    last.then_inc(S["v_ready"], 1)
                    pool.wait_ge(S["qk_mid"], bp.times(1, 1))
                    nc.gpsimd.tensor_tensor(qk_levels[:, :, 2, :], qk_rest[:, :, :], qk_levels[:, :, 1, :], ALU.subtract)\
                        .then_inc(S["qk_low"], 1)

            def causal_step(s):
                before, new = s + -1, s + 3

                def mask_probs(b, n):
                    wait_apart(pool, (S["fill_ready"], 2), (S["f_exp_done"], b.times(4, n + 1)))
                    part = probs_f[:, b.slot(), n * BANK:(n + 1) * BANK]
                    nc.gpsimd.affine_select(out=part, in_=part, compare_op=ALU.is_ge, fill=0.0, base=0,
                                            pattern=[[0, GROUPS], [1, T]], channel_multiplier=-1)\
                        .then_inc(S["f_masked"], 1)

                if live(new):
                    inverse_std(rstd_f, S["f_stats"], S["f_rstd"], new)
                for n in range(4):
                    b, e = lagged(s, n, CAUSAL_LAG, 4)
                    if live(b):
                        mask_probs(b, e)
                    if n == CAUSAL_LAG - 1 and live(new):
                        pool.wait_ge(S["f_q_high"], new.times(1, 1))
                        nc.gpsimd.tensor_tensor(qf_rest[:, :], qf_f[:, :], qf_lev[:, 0, :], ALU.subtract)\
                            .then_inc(S["f_q_resid"], 1)
                        pool.wait_ge(S["f_q_mid"], new.times(1, 1))
                        nc.gpsimd.tensor_tensor(qf_lev[:, 2, :], qf_rest[:, :], qf_lev[:, 1, :], ALU.subtract)\
                            .then_inc(S["f_q_low"], 1)

            schedule(pool, cross_step, causal_step)

        @block.tensor
        def _(pe):
            mm = nc.tensor.matmul

            pe.wait_ge(S["weights_in"], 3 * DMA)
            pe.wait_ge(S["const_ready"], 2)
            for n in range(3):
                last = nc.tensor.transpose(psum[:, BANK_A, n * P:(n + 1) * P], w_rows[:, n, :], ident[:, :])
            last.then_inc(S["w_transposed"], 1)
            pe.wait_ge(S["bias_ordered"], 2)
            for n in range(2):
                last = mm(psum[:, BANK_B, n:n + 1],
                          bias_perm[0:1, n, :], ones_row[0:1, 0:1],
                          start=True, stop=True)
            last.then_inc(S["bias_mm"], 1)
            pe.wait_ge(S["mask_in"], 2 * DMA)
            nc.tensor.transpose(psum[:, BANK_C, 0:B * PT], mask_rows[:, :], ident[0:B * PT, 0:B * PT])\
                .then_inc(S["maskT_mm"], 1)
            pe.wait_ge(S["w_copied"], 3)
            pe.wait_ge(S["bias_copied"], 2)

            def project_qk(b):
                pe.wait_ge(S["xn_ready"], b.times(1, 1))
                pe.wait_ge(in_loaded[b.slot()], b.uses(2 * DMA, 2 * DMA))
                reached(pe, S["qk_copied"], b, 1)
                mm(psum[:, BANK_A, 0:C], wT[:, 0, :], xn[:, :], start=True, stop=True)
                mm(psum[:, BANK_A, C:2 * C], wT[:, 1, :], ctx[:, b.slot(), :], start=True, stop=True)\
                    .then_inc(S["qk_mm"], 1)

            def project_v(b):
                reached(pe, S["v_added"], b, 1)
                for t in range(PT):
                    last = mm(psum[:, BANK_B, t * P:(t + 1) * P], ctx[:, b.slot(), t * P:(t + 1) * P], wT[:, 2, :],
                              start=True, stop=True)
                last.then_inc(S["v_mm"], 1)

            def max_scores(b, h):
                if h == 0:
                    if b.k is None and b.c == 0:
                        pe.wait_ge(S["filled"], 3 * RING * DMA)
                    pe.wait_ge(stack_in[b.slot()], b.uses(STACK_DMAS * DMA, STACK_DMAS * DMA))
                reached(pe, S["max_taken"], b, H, h - 1)
                for t in range(PT):
                    last = mm(psum[:, bank_max[h % 2], t * C:(t + 1) * C],
                              q_stack[0:MAX_ROW, b.slot(RING), h, t * P:(t + 1) * P],
                              k_stack[0:MAX_ROW, b.slot(RING), h, :], start=True, stop=True)
                last.then_inc(S["scores_max"], 1)

            def turn_max(b):
                pe.wait_ge(S["max_split"], b.times(1, 1))
                nc.tensor.transpose(psum[0:LEVELS * H * PT, BANK_C, 0:P // 2].bitcast(BF16), max_levels[:, :],
                                    ident_bf[:, :]).then_inc(S["maxT_mm"], 1)

            def exp_scores(b, h):
                if h == 0:
                    pe.wait_ge(max_in[b.slot()], b.uses(DMA, DMA))
                reached(pe, S["exp_done"], b, H, h - 1)
                for t in range(PT):
                    last = mm(psum[:, bank_exp[h % 2], t * C:(t + 1) * C],
                              k_stack[0:ROWS, b.slot(RING), h, t * P:(t + 1) * P],
                              q_stack[0:ROWS, b.slot(RING), h, :], start=True, stop=True)
                last.then_inc(S["scores_exp"], 1)

            def value_product(b, quad, t):
                region = quad // 2
                if t == 0:
                    pe.wait_ge(S["exp_done"], b.times(H, GROUPS * (quad + 1)))
                    if quad == 0:
                        pe.wait_ge(S["v_ready"], b.times(1, 1))
                        reached(pe, S["pv_copied"], b, 1)
                for j in range(GROUPS):
                    last = mm(psum[j * 32:(j + 1) * 32, BANK_PV, region * C:(region + 1) * C],
                              v_cols[:, b.slot(RING), t, GROUPS * quad + j, :],
                              probs[:, quad % 2, j, t * C:(t + 1) * C],
                              start=(quad % 2 == 0 and t == 0), stop=(quad % 2 == 1 and t == PT - 1),
                              skip_group_check=True)
                if t == PT - 1:
                    last.then_inc(S["pv_done"], 1)

            def turn_outputs(b):
                pe.wait_ge(S["pv_copied"], b.times(1, 1))
                for t in range(PT):
                    for r in range(2):
                        n = t * 2 + r
                        last = nc.tensor.transpose(psum[:, BANK_A, n * P:(n + 1) * P],
                                                   pv_out[:, r * C + t * P:r * C + (t + 1) * P], ident[:, :])
                last.then_inc(S["outT_mm"], 1)

            def turn_back(b):
                pe.wait_ge(S["attn_normed"], b.times(1, 1))
                for t in range(PT):
                    last = nc.tensor.transpose(psum[:, BANK_C, t * P:(t + 1) * P], attn_t[:, t, :], ident[:, :])
                last.then_inc(S["attnT_mm"], 1)

            def turn_ffn_weights():
                pe.wait_ge(S["qkv_in"], 2 * DMA)
                for part, bank in enumerate((bank_exp[0], bank_exp[1], BANK_PV)):
                    for c in range(PT):
                        for t in range(PT):
                            last = nc.tensor.transpose(psum[:, bank, c * C + t * P:c * C + (t + 1) * P],
                                                       wqkv_rows[:, part * PT + t, c * P:(c + 1) * P], ident[:, :])
                for c in range(PT):
                    last = nc.tensor.transpose(psum[:, BANK_C, c * H:(c + 1) * H],
                                               wgate_rows[:, c * P:(c + 1) * P], ident[0:H, 0:H])
                last.then_inc(S["wf_transposed"], 1)

            def cross_step(s):
                before, nxt, new = s + -1, s + 1, s + 3
                if s.k is None and s.c == -1:
                    pe.wait_ge(S["maskcol_ready"], 1)
                    turn_ffn_weights()
                if s.k is None and s.c == 0:
                    pe.wait_ge(S["wf_copied"], 5)
                joined = s.k is None and s.c > JOIN - 3
                for h in range(H):
                    if live(nxt):
                        max_scores(nxt, h)
                    b, e = lagged(s, h, LAG, H)
                    quad, j = divmod(e, GROUPS)
                    if live(b):
                        exp_scores(b, e)
                    if j % 2:
                        b, q = (b + -1, GROUPS - 1) if quad == 0 else (b, quad - 1)
                        if live(b):
                            value_product(b, q, j // 2)
                    if h == 1 and live(s):
                        turn_max(s)
                    if h == LAG and live(new):
                        project_qk(new)
                    if h == 7 and live(new):
                        project_v(new)
                    if h == 11 and live(before):
                        if live(new):
                            pe.wait_ge(S["qk_copied"], new.times(1, 1))
                        if joined:
                            pe.wait_ge(S["f_selected"], s.c - JOIN + 3)
                        turn_outputs(before)
                    if h == 14 and live(before):
                        if joined:
                            pe.wait_ge(S["f_q_copied"], s.c - JOIN + 3)
                        if live(s):
                            pe.wait_ge(S["maxT_copied"], s.times(1, 1))
                        else:
                            pe.wait_ge(S["x_updated"], before.c)
                        turn_back(before)

            def f_turn_x(b):
                pe.wait_ge(S["f_xn"], b.times(1, 1))
                for c in range(PT):
                    last = nc.tensor.transpose(psum[:, BANK_B, c * T:(c + 1) * T], xn_f[:, c * P:(c + 1) * P], ident[:, :])
                last.then_inc(S["f_xnT_mm"], 1)

            def f_project_kv(b):
                if b.c >= 1:
                    pe.wait_ge(S["f_kT"], b.times(1))
                if b.k is None and b.c < 3:
                    pe.wait_ge(S["attn_normed"], b.c + B - 2)
                for c in range(PT):
                    last = mm(psum[:, BANK_A, :], xnT[:, c, :], wfT[:, c, C:3 * C], start=(c == 0), stop=(c == PT - 1))
                last.then_inc(S["f_kv_mm"], 1)

            def f_project_gq(b):
                pe.wait_ge(S["f_xnT"], b.times(1, 1))
                if b.k is None and b.c < 3:
                    pe.wait_ge(S["x_updated"], b.c + B - 2)
                for c in range(PT):
                    mm(psum[:, BANK_C, PT * T:PT * T + H], xnT[:, c, :], wgT[:, c, :], start=(c == 0), stop=(c == PT - 1))
                for t in range(PT):
                    for c in range(PT):
                        last = mm(psum[:, BANK_C, t * T:(t + 1) * T], wfT[:, c, t * P:(t + 1) * P], xnT[:, c, :],
                                  start=(c == 0), stop=(c == PT - 1))
                last.then_inc(S["f_gq_mm"], 1)

            def f_turn_k(b):
                pe.wait_ge(S["f_kT_in"], b.times(1, 1))
                if b.k is None and b.c < 2:
                    pe.wait_ge(S["attn_normed"], b.c + B - 1)
                nc.tensor.transpose(psum[0:ROWS, BANK_A, 0:T // 2].bitcast(BF16), kf_rows[:, :],
                                    ident_bf[:, :]).then_inc(S["f_kT_mm"], 1)

            def f_max_scores(b, n):
                if n == 0:
                    pe.wait_ge(S["f_kT"], b.times(1, 1))
                    pe.wait_ge(f_stack_in[b.slot()], b.uses(len(Q_RUNS) * DMA, len(Q_RUNS) * DMA))
                reached(pe, S["f_max_taken"], b, 4, n - 1)
                bank = bank_max[n % 2]
                mm(psum[:, bank, :].rearrange("p (h t) -> p h t", h=GROUPS), ident_bf[:, :],
                   causal_bf[:, :].unsqueeze(1).to_broadcast([P, GROUPS, T]), start=True, stop=False,
                   skip_group_check=True)
                for j in range(GROUPS):
                    last = mm(psum[:, bank, j * T:(j + 1) * T],
                              q_stack[0:MAX_ROW, b.slot(RING), GROUPS * n + j, 0:T],
                              kf_stack[0:MAX_ROW, b.slot(RING), :], start=False, stop=(j == GROUPS - 1),
                              skip_group_check=True)
                last.then_inc(S["f_scores_max"], 1)

            def f_turn_max(b):
                wait_apart(pe, (S["causal_ready"], 1), (S["f_max_split"], b.times(1, 1)))
                nc.tensor.transpose(psum[0:LEVELS * H, BANK_B, 0:P // 2].bitcast(BF16), maxf_levels[:, :],
                                    ident_bf[:, :]).then_inc(S["f_maxT_mm"], 1)

            def f_exp_scores(b, n):
                if n == 0:
                    pe.wait_ge(f_max_in[b.slot()], b.uses(DMA, DMA))
                reached(pe, S["f_exp_done"], b, 4, n - 1)
                mm(psum[:, bank_exp[n % 2], :], kf_stack[:, b.slot(RING), :],
                   q_stack[:, b.slot(RING), GROUPS * n:GROUPS * (n + 1), 0:T], start=True, stop=True)\
                    .then_inc(S["f_scores_exp"], 1)

            def f_value_product(b):
                pe.wait_ge(S["f_masked"], b.times(4, 4))
                for n in range(GROUPS):
                    last = mm(psum[32 * n:32 * (n + 1), BANK_PV, :], vf_cols[:, b.slot(RING), :],
                              probs_f[:, b.slot(), n * BANK:(n + 1) * BANK], start=True, stop=True)
                last.then_inc(S["f_pv_done"], 1)

            def f_turn_outputs(b):
                pe.wait_ge(S["f_pv_copied"], b.times(1, 1))
                for j in range(GROUPS):
                    last = nc.tensor.transpose(psum[:, BANK_C, j * P:(j + 1) * P], pvf_out[:, j * T:(j + 1) * T],
                                               ident[:, :])
                last.then_inc(S["f_outT_mm"], 1)

            def causal_step(s):
                before, nxt, nxt2, new = s + -1, s + 1, s + 2, s + 3
                if s.k is None and s.c == -3:
                    pe.wait_ge(S["causal_ready"], 1)
                if s.k is None and s.c == -1:
                    pe.wait_ge(S["max_taken"], H * B)
                for n in range(4):
                    if live(nxt):
                        f_max_scores(nxt, n)
                    if n == 2:
                        if live(new):
                            f_project_gq(new)
                            f_project_kv(new)
                        if live(before):
                            f_value_product(before)
                    if n == 3 and live(before):
                        if live(new):
                            pe.wait_ge(S["f_q_copied"], new.times(1, 1))
                        else:
                            reached(pe, S["f_y_ready"], before, 1)
                        f_turn_outputs(before)
                    b, e = lagged(s, n, CAUSAL_LAG, 4)
                    if live(b):
                        f_exp_scores(b, e)
                    if n == 0 and live(s):
                        f_turn_max(s)
                    if n == 1:
                        if live(nxt2):
                            f_turn_k(nxt2)
                        if live(new):
                            if live(s):
                                pe.wait_ge(S["f_maxT_copied"], s.times(1, 1))
                            f_turn_x(new)

            schedule(pe, cross_step, causal_step)

        @block.scalar
        def _(act):
            def copy(dst, src, bias=0.0, scale=1.0, function=ACT.Copy):
                return nc.scalar.activation(dst, src, function, bias=bias, scale=scale)

            act.wait_ge(S["small_in"], 5 * DMA)
            nc.scalar.activation(gates[:, :], gates_in[:, :], ACT.Tanh).then_inc(S["tanh_done"], 1)
            for n, scale in enumerate((XATTN_SCALE, 1.0)):
                copy(bias_perm[:, n, :].rearrange("a (d h) -> a d h", h=H),
                     bias_rows[:, n, :].rearrange("a (h d) -> a d h", d=DX), scale=scale).then_inc(S["bias_ordered"], 1)
            act.wait_ge(S["bias_mm"], 1)
            copy(bias_col[:, 0:1], psum[:, BANK_B, 0:1]).then_inc(S["bias_copied"], 1)
            copy(bias_col[:, 1:2], psum[:, BANK_B, 1:2]).then_inc(S["bias_copied"], 1)
            act.wait_ge(S["maskT_mm"], 1)
            copy(mask_col[:, :], psum[:, BANK_C, 0:B * PT]).then_inc(S["maskcol_ready"], 1)

            def cross_step(s):
                before, nxt, new = s + -1, s + 1, s + 3

                def copy_max(b):
                    act.wait_ge(S["maxT_mm"], b.times(1, 1))
                    if b.c >= 1:
                        last = b + -1
                        act.wait_ge(max_in[last.slot()], last.uses(DMA, DMA))
                    copy(max_rows[:, :], psum[0:LEVELS * H * PT, BANK_C, 0:P // 2].bitcast(BF16))\
                        .then_inc(S["maxT_copied"], 1)

                if s.k is None and s.c == -1:
                    act.wait_ge(S["wf_transposed"], 1)
                    for c in range(PT):
                        copy(wfT[:, c, 0:C].rearrange("p (d h) -> p h d", h=H),
                             psum[:, bank_exp[0], c * C:(c + 1) * C].rearrange("p (h d) -> p h d", h=H),
                             scale=FFN_SCALE).then_inc(S["wf_copied"], 1)
                    for n, bank in enumerate((bank_exp[1], BANK_PV)):
                        copy(wfT[:, :, (n + 1) * C:(n + 2) * C],
                             psum[:, bank, :].rearrange("p (c o) -> p c o", c=PT)).then_inc(S["wf_copied"], 1)
                    copy(wgT[:, :, :], psum[:, BANK_C, 0:PT * H].rearrange("p (c h) -> p c h", c=PT))\
                        .then_inc(S["wf_copied"], 1)
                for h in range(H):
                    b, e = lagged(s, h, LAG, H)
                    quad, j = divmod(e, GROUPS)
                    if live(b):
                        act.wait_ge(S["scores_exp"], b.times(H, e + 1))
                        if j == 0:
                            reached(act, S["pv_done"], b, 4, quad - 1)
                        nc.scalar.activation(probs[:, quad % 2, j, :], psum[:, bank_exp[e % 2], :], ACT.Exp)\
                            .then_inc(S["exp_done"], 1)
                    if h == 1 and live(s):
                        copy_max(s)
                    if h == 10 and live(before):
                        act.wait_ge(S["pv_done"], before.times(4, 4))
                        copy(pv_out[:, :], psum[:, BANK_PV, :]).then_inc(S["pv_copied"], 1)
                    if h == LAG and live(new):
                        act.wait_ge(S["qk_mm"], new.times(1, 1))
                        if s.k is None and s.c == -3:
                            act.wait_ge(S["bias_copied"], 2)
                        for n in range(2):
                            last = copy(qk_raw[:, n, :], psum[:, BANK_A, n * C:(n + 1) * C], bias=bias_col[:, n:n + 1],
                                        function=ACT.Identity)
                        last.then_inc(S["qk_copied"], 1)
                    if h == 8 and live(new):
                        act.wait_ge(S["qk_masked"], new.times(1, 1))
                        if new.c >= 1:
                            last = new + -1
                            act.wait_ge(levels_out[last.slot()], last.uses(DMA, DMA))
                        copy(qk_levels[:, :, 0, :], qk_f[:, :, :]).then_inc(S["qk_high"], 1)
                    if h == 11 and live(new):
                        act.wait_ge(S["qk_resid"], new.times(1, 1))
                        copy(qk_levels[:, :, 1, :], qk_rest[:, :, :]).then_inc(S["qk_mid"], 1)

            def causal_step(s):
                before, nxt, nxt2, new = s + -1, s + 1, s + 2, s + 3

                def copy_max(b):
                    act.wait_ge(S["f_maxT_mm"], b.times(1, 1))
                    if b.c >= 1:
                        last = b + -1
                        act.wait_ge(f_max_in[last.slot()], last.uses(DMA, DMA))
                    copy(maxf_rows[:, :], psum[0:LEVELS * H, BANK_B, 0:P // 2].bitcast(BF16))\
                        .then_inc(S["f_maxT_copied"], 1)

                for n in range(4):
                    b, e = lagged(s, n, CAUSAL_LAG, 4)
                    if live(b):
                        act.wait_ge(S["f_scores_exp"], b.times(4, e + 1))
                        nc.scalar.activation(probs_f[:, b.slot(), e * BANK:(e + 1) * BANK], psum[:, bank_exp[e % 2], :],
                                             ACT.Exp).then_inc(S["f_exp_done"], 1)
                    if n == 0 and live(s):
                        copy_max(s)
                    if n == 1:
                        if live(nxt2):
                            act.wait_ge(S["f_kT_mm"], nxt2.times(1, 1))
                            copy(kf_stack[:, nxt2.slot(RING), :],
                                 psum[0:ROWS, BANK_A, 0:T // 2].bitcast(BF16)).then_inc(S["f_kT"], 1)
                        if live(new):
                            act.wait_ge(S["f_xnT_mm"], new.times(1, 1))
                            copy(xnT[:, :, :], psum[:, BANK_B, 0:PT * T].rearrange("p (c t) -> p c t", c=PT))\
                                .then_inc(S["f_xnT"], 1)
                            act.wait_ge(S["f_gq_mm"], new.times(1, 1))
                            reached(act, S["f_q_low"], new, 1)
                            copy(logit[:, :], psum[:, BANK_C, PT * T:PT * T + H])
                            copy(qf_f[:, :], psum[:, BANK_C, 0:PT * T]).then_inc(S["f_q_copied"], 1)
                            act.wait_ge(S["f_q_copied"], new.times(1, 1))
                            if new.c >= 1:
                                last = new + -1
                                act.wait_ge(f_levels_out[last.slot()], last.uses(PT * DMA, PT * DMA))
                            copy(qf_lev[:, 0, :], qf_f[:, :]).then_inc(S["f_q_high"], 1)
                        if live(before):
                            act.wait_ge(S["f_pv_done"], before.times(1, 1))
                            copy(pvf_out[:, :], psum[:, BANK_PV, :]).then_inc(S["f_pv_copied"], 1)
                        if live(new):
                            act.wait_ge(S["f_logit"], new.times(1, 1))
                            nc.scalar.activation(gate_e[:, :], logit[:, :], ACT.Exp, bias=top_neg[:, 0:1],
                                                 accum_out=gate_sum[:, 0:1]).then_inc(S["f_gate_e"], 1)
                            act.wait_ge(S["f_q_resid"], new.times(1, 1))
                            copy(qf_lev[:, 1, :], qf_rest[:, :]).then_inc(S["f_q_mid"], 1)

            schedule(act, cross_step, causal_step)

        @block.vector
        def _(dve):
            chain = Chain(dve, S["dve_chain"])
            v = nc.vector

            v.memset(zero_rows[:, :, :], 0.0).then_inc(S["fill_ready"], 1)
            dve.wait_ge(S["w_transposed"], 1)
            v.tensor_scalar(wT[:, 0, :].rearrange("p (d h) -> p h d", h=H),
                            psum[:, BANK_A, 0:P].rearrange("p (h d) -> p h d", h=H),
                            XATTN_SCALE, None, ALU.mult).then_inc(S["w_copied"], 1)
            v.tensor_copy(wT[:, 1, :].rearrange("p (d h) -> p h d", h=H),
                          psum[:, BANK_A, P:2 * P].rearrange("p (h d) -> p h d", h=H)).then_inc(S["w_copied"], 1)
            v.tensor_copy(wT[:, 2, :], psum[:, BANK_A, 2 * P:3 * P]).then_inc(S["w_copied"], 1)
            dve.wait_ge(S["mask_in"], 2 * DMA)
            v.tensor_copy(aug_f[:, 0, :], mask_b[:, :])
            chain(v.tensor_scalar(aug_f[:, 1, :], mask_b[:, :], 1.0, NEG, ALU.subtract, ALU.mult))
            chain(v.tensor_copy(aug_levels[:, :, 0, :], aug_f[:, :, :]))
            chain(v.tensor_tensor(aug_r[:, :, :], aug_f[:, :, :], aug_levels[:, :, 0, :], ALU.subtract))
            chain(v.tensor_copy(aug_levels[:, :, 1, :], aug_r[:, :, :]))
            v.tensor_tensor(aug_levels[:, :, 2, :], aug_r[:, :, :], aug_levels[:, :, 1, :], ALU.subtract)\
                .then_inc(S["aug_ready"], 1)
            dve.wait_ge(S["maskcol_ready"], 1)
            dve.wait_ge(S["tanh_done"], 1)
            chain(v.tensor_scalar(mask_gate[:, :], mask_col[:, :], gates[:, 0:1], None, ALU.mult))
            dve.wait_ge(S["small_in"], 5 * DMA)

            def split_max(neg, levels, rest, signal):
                n = neg.shape[1]
                chain(v.tensor_copy(levels[:, 0:n], neg))
                chain(v.tensor_tensor(rest, neg, levels[:, 0:n], ALU.subtract))
                chain(v.tensor_copy(levels[:, n:2 * n], rest))
                v.tensor_tensor(levels[:, 2 * n:3 * n], rest, levels[:, n:2 * n], ALU.subtract).then_inc(signal, 1)

            def moments(b, st, mv, r, signal):
                v.bn_stats(st[:, :], xs[:, b.index, :]).then_inc(S["dve_chain"], 1)
                chain.n += 1
                wait_apart(dve, (S["tanh_done"], 1), (S["dve_chain"], chain.base + chain.n))
                chain(v.bn_aggr(mv[:, :], st[:, :]))
                v.tensor_scalar(r[:, 0:1], mv[:, 1:2], EPS, None, ALU.add).then_inc(signal, 1)

            def normalise(b, dst, mv, r, signal):
                v.tensor_scalar(dst[:, :], xs[:, b.index, :], mv[:, 0:1], r[:, 1:2], ALU.subtract, ALU.mult)\
                    .then_inc(signal, 1)

            def normalise_outputs(b):
                dve.wait_ge(S["outT_mm"], b.times(1, 1))
                rows = psum[:, BANK_A, :].rearrange("p (g j x) -> p g j x", g=2 * PT, j=GROUPS)
                chain(v.reciprocal(recip[:, :].rearrange("p (g j s) -> p g j s", g=2 * PT, j=GROUPS),
                                   rows[:, :, :, 2 * DX:2 * DX + 2]))
                chain(v.tensor_tensor(recip_g[:, :].rearrange("p (t n) -> p t n", t=PT),
                                      recip[:, :].rearrange("p (t n) -> p t n", t=PT),
                                      mask_gate[:, bass.ds(b.times(PT), PT)].unsqueeze(2).to_broadcast([P, PT, 2 * 8]),
                                      ALU.mult))
                dst = attn_t[:, :, :].rearrange("p t (r s j d) -> p (t r) s j d", r=2, s=2, j=GROUPS)
                scale = recip_g[:, :].rearrange("p (g j s) -> p g j s", g=2 * PT, j=GROUPS)
                for slot in range(2):
                    last = v.tensor_tensor(dst[:, :, slot, :, :], rows[:, :, :, slot * DX:(slot + 1) * DX],
                                           scale[:, :, :, slot].unsqueeze(3).to_broadcast([P, 2 * PT, GROUPS, DX]),
                                           ALU.mult)
                last.then_inc(S["attn_normed"], 1)

            def cross_step(s):
                before, nxt, new = s + -1, s + 1, s + 3
                if live(s):
                    dve.wait_ge(S["max_taken"], s.times(H, H))
                    split_max(neg_max[:, :], max_levels, max_rest[:, :], S["max_split"])
                for h in range(H):
                    if live(nxt):
                        dve.wait_ge(S["scores_max"], nxt.times(H, h + 1))
                        v.tensor_reduce(out=neg_max[:, h * PT:(h + 1) * PT], in_=psum[:, bank_max[h % 2], :]
                                        .rearrange("p (t c) -> p t c", t=PT), op=ALU.max, axis=AX.X, negate=True)\
                            .then_inc(S["max_taken"], 1)
                    if h == 0 and live(new):
                        if s.k is None and s.c == -3:
                            dve.wait_ge(S["x_first"], DMA)
                        if s.k is None and s.c == 0:
                            dve.wait_ge(S["x_rest"], DMA)
                        moments(new, stats, meanvar, rstd, S["norm_stats"])
                    if h == 2 and live(new):
                        dve.wait_ge(S["rstd_ready"], new.times(1, 1))
                        normalise(new, xn, meanvar, rstd, S["xn_ready"])
                    if h == 9 and live(new):
                        dve.wait_ge(S["v_mm"], new.times(1, 1))
                        reached(dve, S["v_ready"], new, 1)
                        v.tensor_tensor(v_sum[:, :, :], psum[:, BANK_B, 0:PT * P].rearrange("p (t o) -> p t o", t=PT),
                                        bv_all[:, :].unsqueeze(1).to_broadcast([P, PT, P]), ALU.add)\
                            .then_inc(S["v_added"], 1)
                    if h == 12 and live(before):
                        normalise_outputs(before)
                    if h == 15 and live(before):
                        dve.wait_ge(S["attnT_mm"], before.times(1, 1))
                        v.tensor_tensor(xs[:, before.index, :], psum[:, BANK_C, 0:C], xs[:, before.index, :], ALU.add)\
                            .then_inc(S["x_updated"], 1)

            def choose_head(b):
                dve.wait_ge(S["f_q_copied"], b.times(1, 1))
                v.tensor_reduce(out=top_neg[:, 0:1], in_=logit[:, :], op=ALU.max, axis=AX.X, negate=True)\
                    .then_inc(S["f_logit"], 1)
                dve.wait_ge(S["f_logit"], b.times(1, 1))
                chain(v.tensor_scalar(rank[:, :], logit[:, :], top_neg[:, 0:1], 0.0, ALU.add, ALU.is_ge))
                chain(v.tensor_tensor(rank[:, :], rank[:, :], first_head[:, :], ALU.mult))
                chain(v.tensor_reduce(out=rank_top[:, :], in_=rank[:, :], op=ALU.max, axis=AX.X))
                chain(v.tensor_scalar(chosen[:, :], rank[:, :], rank_top[:, 0:1], None, ALU.is_ge))

            def select_head(b):
                dve.wait_ge(S["f_kv_mm"], b.times(1, 1))
                v.tensor_tensor(kv_sel[:, :, :, :], psum[:, BANK_A, :].rearrange("p (k h d) -> p k h d", k=2, h=H),
                                chosen[:, :].unsqueeze(1).unsqueeze(3).to_broadcast([P, 2, H, DF]), ALU.mult)\
                    .then_inc(S["f_selected"], 1)
                dve.wait_ge(S["f_selected"], b.times(1, 1))
                chain(v.tensor_reduce(out=kv_one[:, :, :], in_=kv_sel[:, :, :, :].rearrange("p k h d -> p k d h"),
                                      op=ALU.add, axis=AX.X))

            def lay_out_k(b):
                k_rows = kf_rows[:, 0:MAX_ROW].rearrange("p (g d) -> p g d", d=DF)
                kk = kv_one[:, 0, :].unsqueeze(1)
                chain(v.tensor_copy(k_rows[:, 0:3, :], kk.to_broadcast([P, 3, DF])))
                chain(v.tensor_tensor(kf_rest[:, :, :], kk.to_broadcast([P, 2, DF]), k_rows[:, 0:2, :], ALU.subtract))
                chain(v.tensor_copy(k_rows[:, 3:5, :], kf_rest[:, :, :]))
                v.tensor_tensor(k_rows[:, 5, :], kf_rest[:, 0, :], k_rows[:, 3, :], ALU.subtract).then_inc(S["f_kT_in"], 1)
                dve.wait_ge(S["f_gate_e"], b.times(1, 1))
                chain(v.reciprocal(gate_sum[:, 1:2], gate_sum[:, 0:1]))
                v.tensor_scalar(vf_cols[:, b.slot(RING), 0:DF], kv_one[:, 1, :], gate_sum[:, 1:2], None, ALU.mult)\
                    .then_inc(S["f_v_ready"], 1)

            def finish(b):
                dve.wait_ge(S["f_outT_mm"], b.times(1, 1))
                rows = psum[:, BANK_C, :].rearrange("p (j g x) -> p j g x", j=GROUPS, g=GROUPS)
                chain(v.reciprocal(recip_f[:, :].rearrange("p (j g) -> p j g", j=GROUPS), rows[:, :, :, DF]))
                chain(v.tensor_scalar(recip_fg[:, :], recip_f[:, :], gates[:, 1:2], None, ALU.mult))
                v.tensor_tensor(y_f[:, :].rearrange("p (g j d) -> p j g d", g=GROUPS, j=GROUPS), rows[:, :, :, 0:DF],
                                recip_fg[:, :].rearrange("p (j g) -> p j g", j=GROUPS).unsqueeze(3)
                                .to_broadcast([P, GROUPS, GROUPS, DF]), ALU.mult).then_inc(S["f_y_ready"], 1)
                dve.wait_ge(S["f_y_ready"], b.times(1, 1))
                v.tensor_tensor(xs[:, b.index, :], y_f[:, :], xs[:, b.index, :], ALU.add).then_inc(S["f_out_ready"], 1)

            def causal_step(s):
                before, nxt, new = s + -1, s + 1, s + 3
                if s.k is None and s.c == -3:
                    dve.wait_ge(S["causal_ready"], 1)
                if live(s):
                    dve.wait_ge(S["f_max_taken"], s.times(4, 4))
                    split_max(neg_max_f[:, :], maxf_levels, maxf_rest[:, :], S["f_max_split"])
                for n in range(4):
                    if live(nxt):
                        dve.wait_ge(S["f_scores_max"], nxt.times(4, n + 1))
                        v.tensor_reduce(out=neg_max_f[:, n * GROUPS:(n + 1) * GROUPS], in_=psum[:, bank_max[n % 2], :]
                                        .rearrange("p (h t) -> p h t", h=GROUPS), op=ALU.max, axis=AX.X, negate=True)\
                            .then_inc(S["f_max_taken"], 1)
                    if n == 0 and live(new):
                        moments(new, stats_f, meanvar_f, rstd_f, S["f_stats"])
                    if n == 1 and live(new):
                        dve.wait_ge(S["f_rstd"], new.times(1, 1))
                        normalise(new, xn_f, meanvar_f, rstd_f, S["f_xn"])
                    if n == 2 and live(new):
                        choose_head(new)
                        select_head(new)
                        lay_out_k(new)
                if live(before):
                    finish(before)

            schedule(dve, cross_step, causal_step, chain, 7, 16)


_INS = ['x', 'ctx_2048', 'mask_Bx1x2048_fk1', 'g_xattn', 'g_ffn', 'L0_xattn_Wq', 'L0_xattn_bq', 'L0_xattn_Wk',
        'L0_xattn_bk', 'L0_xattn_Wv', 'L0_xattn_bv', 'L0_ffn_W_gate', 'L0_ffn_W_qkv']


def kernel(**inputs):
    import numpy as _np
    import concourse.bacc as _bacc
    from concourse import mybir as _mybir
    from concourse.bass_utils import run_bass_kernel_spmd as _run

    nc = _bacc.Bacc("TRN2", target_bir_lowering=False, num_devices=1)
    arrays, args = {}, []
    for name in _INS:
        a = _np.ascontiguousarray(inputs[name])
        arrays[f"in_{name}"] = a
        args.append(nc.dram_tensor(f"in_{name}", a.shape, _mybir.dt.from_np(a.dtype), kind="ExternalInput").ap())
    x = inputs["x"]
    out = nc.dram_tensor("out", x.shape, _mybir.dt.float32, kind="ExternalOutput").ap()
    flamingo_kernel(nc, *args, out)
    r = _run(nc, [arrays], core_ids=[0])
    return r.results[0]["out"]
```

```python
from contextlib import ExitStack

import concourse.bass as bass
from concourse import mybir

F32 = mybir.dt.float32
BF16 = mybir.dt.bfloat16
ALU = mybir.AluOpType
ACT = mybir.ActivationFunctionType
AX = mybir.AxisListType

P = 128
LEVELS = 3
BANK = 512
EPS = 1e-5
NEG = 1000000.0

PAIRS = [(0, 0), (1, 0), (2, 0), (0, 1), (1, 1), (0, 2)]
Q_RUNS = [(0, 0, 3), (3, 0, 2), (5, 0, 1)]
K_RUNS = [(0, 0, 3), (3, 1, 2), (5, 2, 1)]
MAX_ROW = 96
ROWS = MAX_ROW + LEVELS
RING = 4
LAG = 7
DMA = 16


class Batch:

    def __init__(self, c, k=None, m=0):
        self.c, self.k, self.m = c, k, m

    def __add__(self, n):
        return Batch(self.c + n, self.k, self.m)

    def times(self, f, extra=0):
        return f * self.c + extra if self.k is None else self.k * (f * self.m) + (f * self.c + extra)

    def uses(self, f, extra=0, ring=2):
        n = f * (self.c // ring) + extra
        assert n > 0
        return n if self.k is None else self.k * (f * self.m // ring) + n

    @property
    def index(self):
        return self.times(1)

    def slot(self, ring=2):
        return self.c % ring


def reached(eng, semaphore, b, per_batch, extra=0):
    first = per_batch * b.c + extra
    if b.k is None:
        if first > 0:
            eng.wait_ge(semaphore, first)
    else:
        assert first > 0
        eng.wait_ge(semaphore, b.times(per_batch, extra))


def wait_apart(eng, held, *waits):
    values = [(semaphore, v if isinstance(v, int) else eng.to_reg(v)) for semaphore, v in waits]
    eng.wait_ge(*held)
    for semaphore, v in values:
        if not isinstance(v, int) or v > 0:
            eng.wait_ge(semaphore, v)


class Chain:

    def __init__(self, eng, sem):
        self.eng, self.sem, self.base, self.n = eng, sem, 0, 0

    def mark(self, instruction):
        instruction.then_inc(self.sem, 1)
        self.n += 1
        return self.n

    def passed(self, mark):
        self.eng.wait_ge(self.sem, self.base + mark)

    def __call__(self, instruction):
        self.passed(self.mark(instruction))

    def enter(self, k, per_turn):
        self.start = self.base + self.n
        self.base, self.n, self.per_turn = k * per_turn + self.start, 0, per_turn

    def leave(self, turns):
        assert self.n == self.per_turn, (self.n, self.per_turn)
        self.base, self.n = self.start + turns * self.per_turn, 0


def flamingo_kernel(nc, x, ctx_in, mask, g_xattn, g_ffn, Wq, bq, Wk, bk, Wv, bv, W_gate, W_qkv, out):
    B, T, C = x.shape
    H = W_gate.shape[0]
    DX = T // H
    DF = C // H
    PT = C // P
    GROUPS = 4
    CHX = DX + 1
    PAIR_ROWS_X = len(PAIRS) * CHX
    assert T == P and C == PT * P and PAIR_ROWS_X <= MAX_ROW and len(PAIRS) * DF == MAX_ROW
    assert P // GROUPS >= 2 * DX + 2 and H == GROUPS * GROUPS
    XATTN_SCALE = float(DX) ** -0.5
    FFN_SCALE = float(DF) ** -0.5

    levels = nc.dram_tensor("levels", (B, 2, LEVELS, CHX, H, C), BF16).ap()
    qf_levels = nc.dram_tensor("qf_levels", (B, LEVELS, DF, H, T), BF16).ap()

    with ExitStack() as stack:
        def sb(name, shape, dt=F32):
            return stack.enter_context(nc.sbuf_tensor(name, shape, dt))

        def sem(name):
            return stack.enter_context(nc.semaphore(name))

        psum = stack.enter_context(nc.psum_tensor("psum", [P, 8, BANK], F32))
        BANK_PV, BANK_A, BANK_B, BANK_C = 4, 5, 6, 7
        bank_max = [0, 1, BANK_A, BANK_B]
        bank_exp = [2, 3]
        CAUSAL_MAX_BANKS = 2

        ident = sb("ident", [P, P])
        ident_bf = sb("ident_bf", [P, P], BF16)
        causal_bf = sb("causal_bf", [P, P], BF16)
        ones_row = sb("ones_row", [1, P])
        half_power = sb("half_power", [P, 1])
        first_head = sb("first_head", [P, H])
        w_rows = sb("w_rows", [P, 3, P])
        wqkv_rows = sb("wqkv_rows", [P, 3 * C // P, C])
        wgate_rows = sb("wgate_rows", [H, C])
        wT = sb("wT", [P, 3, P])
        bias_rows = sb("bias_rows", [1, 2, P])
        bias_perm = sb("bias_perm", [1, 2, P])
        bias_col = sb("bias_col", [P, 2])
        bv_all = sb("bv_all", [P, P])
        gates_in = sb("gates_in", [P, 2])
        gates = sb("gates", [P, 2])
        mask_rows = sb("mask_rows", [B * PT, P])
        mask_col = sb("mask_col", [P, B * PT])
        mask_gate = sb("mask_gate", [P, B * PT])
        mask_b = sb("mask_b", [B, C])
        aug_f = sb("aug_f", [B, 2, C])
        aug_r = sb("aug_r", [B, 2, C])
        aug_levels = sb("aug_levels", [B, 2, LEVELS, C], BF16)
        wfT = sb("wfT", [P, PT, 3 * C])
        wgT = sb("wgT", [P, PT, H])

        xs = sb("xs", [P, B, C])
        ctx = sb("ctx", [P, 2, C])
        mask_all = sb("mask_all", [P, 2, C])
        stats = sb("stats", [P, 2, 6])
        meanvar = sb("meanvar", [P, 2, 2])
        rstd = sb("rstd", [P, 2, 2])
        xn = sb("xn", [P, C])
        qk_raw = sb("qk_raw", [P, 2, C])
        qk_f = sb("qk_f", [P, 2, C])
        qk_rest = sb("qk_rest", [P, 2, C])
        qk_levels = sb("qk_levels", [P, 2, LEVELS, C], BF16)
        v_sum = sb("v_sum", [P, PT, P])
        v_cols = sb("v_cols", [P, RING, PT, H, 32])
        q_stack = sb("q_stack", [ROWS, RING, H, C], BF16)
        k_stack = sb("k_stack", [ROWS, RING, H, C], BF16)
        zero_rows = sb("zero_rows", [MAX_ROW - PAIR_ROWS_X, 4 * C], BF16)
        one_rows = sb("one_rows", [LEVELS, C], BF16)
        neg_max = sb("neg_max", [P, 2, H * PT])
        max_rest = sb("max_rest", [P, H * PT])
        max_levels = sb("max_levels", [P, LEVELS * H * PT], BF16)
        max_rows = sb("max_rows", [LEVELS * H * PT, P], BF16)
        probs = sb("probs", [P, 2, GROUPS, PT * C])
        pv_out = sb("pv_out", [P, 2 * C])
        recip = sb("recip", [P, 32])
        recip_g = sb("recip_g", [P, 32])
        attn_t = sb("attn_t", [P, PT, P])

        stats_f = sb("stats_f", [P, 6])
        meanvar_f = sb("meanvar_f", [P, 2])
        rstd_f = sb("rstd_f", [P, 2])
        xn_f = sb("xn_f", [P, C])
        xnT = sb("xnT", [P, PT, T])
        qf_f = sb("qf_f", [P, PT * T])
        qf_rest = sb("qf_rest", [P, PT * T])
        qf_lev = sb("qf_lev", [P, LEVELS, PT * T], BF16)
        logit = sb("logit", [P, H])
        top_neg = sb("top_neg", [P, 2])
        gate_e = sb("gate_e", [P, H])
        gate_sum = sb("gate_sum", [P, 2])
        rank = sb("rank", [P, H])
        rank_top = sb("rank_top", [P, 1])
        chosen = sb("chosen", [P, H])
        kv_sel = sb("kv_sel", [P, 2, H, DF])
        kv_one = sb("kv_one", [P, 2, DF])
        kf_rest = sb("kf_rest", [P, 2, DF])
        kf_rows = sb("kf_rows", [P, ROWS], BF16)
        vf_cols = sb("vf_cols", [P, RING, P // GROUPS])
        kf_stack = sb("kf_stack", [ROWS, RING, T], BF16)
        neg_max_f = sb("neg_max_f", [P, H])
        maxf_rest = sb("maxf_rest", [P, H])
        maxf_levels = sb("maxf_levels", [P, LEVELS * H], BF16)
        maxf_rows = sb("maxf_rows", [LEVELS * H, P], BF16)
        probs_f = sb("probs_f", [P, 2, H * T])
        pvf_out = sb("pvf_out", [P, BANK])
        recip_f = sb("recip_f", [P, H])
        recip_fg = sb("recip_fg", [P, H])
        y_f = sb("y_f", [P, C])

        S = {}
        for name in (
            "weights_in x_first x_second x_rest bias_in gates_in bv_in maskrow_in mask_in qkv_in "
            "const_ready pool_chain dve_chain fill_ready filled_0 filled_1 filled_rest causal_ready w_transposed w_copied "
            "wf_transposed wf_copied "
            "bias_ordered bias_mm bias_copied tanh_done aug_ready maskT_mm maskcol_ready aug_written vcols_zero vcols_ready "
            "norm_stats rstd_ready xn_ready qk_mm v_mm qk_copied v_added qk_masked qk_high qk_resid qk_mid qk_low v_ready "
            "scores_max max_taken max_split maxT_mm maxT_copied scores_exp exp_done pv_done pv_copied "
            "outT_mm attn_normed attnT_mm x_updated "
            "f_stats f_rstd f_xn f_xnT_mm f_xnT f_kv_mm f_gq_mm f_logit f_gate_e f_selected f_q_copied f_q_high f_q_resid f_q_mid "
            "f_q_low f_kT_in f_kT_mm f_kT f_scores_max f_max_taken f_max_split f_maxT_mm f_maxT_copied f_scores_exp "
            "f_exp_done f_masked f_pv_done f_pv_copied f_outT_mm f_y_ready f_out_ready"
        ).split():
            S[name] = sem(name)
        in_loaded = [sem(f"in_loaded{i}") for i in range(2)]
        levels_out = [sem(f"levels_out{i}") for i in range(2)]
        stack_in = [sem(f"stack_in{i}") for i in range(2)]
        max_in = [sem(f"max_in{i}") for i in range(2)]
        f_levels_out = [sem(f"f_levels_out{i}") for i in range(2)]
        f_stack_in = [sem(f"f_stack_in{i}") for i in range(2)]
        f_max_in = [sem(f"f_max_in{i}") for i in range(2)]
        out_written = sem("out_written")
        STACK_DMAS = len(Q_RUNS) + len(K_RUNS)

        def schedule(eng, cross_step, causal_step, chain=None, cross_per_step=0, causal_per_step=0):
            unroll = RING
            turns = (B - 4) // unroll
            assert turns * unroll == B - 4
            for step, per_step, joined in ((cross_step, cross_per_step, 0), (causal_step, causal_per_step, 3)):
                for s in range(-3 + joined, 1):
                    step(Batch(s))
                with eng.Fori(0, turns) as k:
                    if chain:
                        chain.enter(k, per_step * unroll)
                    for u in range(unroll):
                        step(Batch(1 + u, k, unroll))
                if chain:
                    chain.leave(turns)
                for s in range(B - 3, B + 1):
                    step(Batch(s))

        JOIN = B + 1
        JOIN_HEAD = 11

        def joins(s, h, place):
            return s.k is None and s.c - JOIN >= -3 and h == (place if s.c - JOIN > -3 or place < JOIN_HEAD else H - 1)

        def moments_due(s):
            if s.k is not None:
                return [s + 3]
            return {-3: [Batch(0), Batch(1)], -2: [Batch(2)], -1: [Batch(3)]}.get(s.c, [])

        def live(b):
            return b.k is not None or 0 <= b.c < B

        def lagged(s, n, lag, per_batch):
            return (s + -1, n - lag + per_batch) if n < lag else (s, n - lag)

        block = stack.enter_context(nc.Block())

        @block.sync
        def _(sp):
            def load_x(first, last, signal):
                sp.dma_start(xs[:, first:last, :], x[first:last].rearrange("b t c -> t b c")).then_inc(signal, DMA)

            load_x(0, 2, S["x_first"])
            for n, w in enumerate((Wq, Wk, Wv)):
                sp.dma_start(w_rows[:, n, :], w).then_inc(S["weights_in"], DMA)
            for n, v in enumerate((bq, bk)):
                sp.dma_start(bias_rows[:, n, :], v.rearrange("(a n) -> a n", a=1)).then_inc(S["bias_in"], DMA)
            sp.dma_start(ctx[:, 0, :], ctx_in[0]).then_inc(in_loaded[0], DMA)
            sp.dma_start(mask_all[:, 0, :], mask[0].to_broadcast([P, C])).then_inc(in_loaded[0], DMA)
            sp.dma_start(mask_b[:, :], mask.rearrange("b a c -> (b a) c")).then_inc(S["mask_in"], DMA)
            sp.dma_start(bv_all[:, :], bv.rearrange("(a n) -> a n", a=1).to_broadcast([P, P])).then_inc(S["bv_in"], DMA)
            sp.dma_start(mask_rows[:, :], mask.rearrange("b a (t p) -> (b a t) p", p=P)).then_inc(S["maskrow_in"], DMA)
            for n, v in enumerate((g_xattn, g_ffn)):
                sp.dma_start(gates_in[:, n:n + 1], v.rearrange("(a n) -> a n", a=1).to_broadcast([P, 1]))\
                    .then_inc(S["gates_in"], DMA)
            sp.dma_start(ctx[:, 1, :], ctx_in[1]).then_inc(in_loaded[1], DMA)
            sp.dma_start(mask_all[:, 1, :], mask[1].to_broadcast([P, C])).then_inc(in_loaded[1], DMA)
            load_x(2, 4, S["x_second"])

            sp.wait_ge(S["aug_ready"], 1)
            for side in range(2):
                for l in range(LEVELS):
                    sp.dma_start(levels[:, side, l, DX], aug_levels[:, side, l].unsqueeze(1).to_broadcast([B, H, C]))\
                        .then_inc(S["aug_written"], DMA)

            sp.wait_ge(S["fill_ready"], 2)

            def fill(i):
                filled = S[("filled_0", "filled_1", "filled_rest", "filled_rest")[i]]
                for st in (k_stack, q_stack):
                    sp.dma_start(st[PAIR_ROWS_X:MAX_ROW, i, :, :],
                                 zero_rows[:, :].unsqueeze(1).to_broadcast([MAX_ROW - PAIR_ROWS_X, H // 4, 4 * C]))\
                        .then_inc(filled, DMA)
                sp.dma_start(k_stack[MAX_ROW:ROWS, i, :, :], one_rows[:, :].unsqueeze(1).to_broadcast([LEVELS, H, C]))\
                    .then_inc(filled, DMA)

            fill(0)

            loaded = (S["weights_in"], 3 * DMA)

            def load_inputs(b):
                if not live(b):
                    return
                wait_apart(sp, loaded, (S["v_mm"], b.times(1, -1)), (S["qk_masked"], b.times(1, -1)))
                sp.dma_start(ctx[:, b.slot(), :], ctx_in[b.index]).then_inc(in_loaded[b.slot()], DMA)
                sp.dma_start(mask_all[:, b.slot(), :], mask[b.index].to_broadcast([P, C]))\
                    .then_inc(in_loaded[b.slot()], DMA)

            def write_levels(b):
                if not live(b):
                    return
                wait_apart(sp, loaded, (S["qk_low"], b.times(1, 1)))
                sp.dma_start(levels[b.index][:, :, 0:DX].rearrange("s l d h c -> (d h) s l c"), qk_levels[:, :, :, :])\
                    .then_inc(levels_out[b.slot()], DMA)

            def load_stack(b):
                if not live(b):
                    return
                wait_apart(sp, loaded, (levels_out[b.slot()], b.uses(DMA, DMA)), (S["aug_written"], 2 * LEVELS * DMA))
                for pair, level, n in Q_RUNS:
                    sp.dma_start(q_stack[pair * CHX:(pair + n) * CHX, b.slot(RING), :, :],
                                 levels[b.index][0, level:level + n]).then_inc(stack_in[b.slot()], DMA)
                for pair, level, n in K_RUNS:
                    sp.dma_start(k_stack[pair * CHX:(pair + n) * CHX, b.slot(RING), :, :],
                                 levels[b.index][1, level:level + 1].to_broadcast([n, CHX, H, C]))\
                        .then_inc(stack_in[b.slot()], DMA)

            def load_max(b):
                if not live(b):
                    return
                wait_apart(sp, loaded, (S["maxT_copied"], b.times(1, 1)))
                sp.dma_start(q_stack[MAX_ROW:ROWS, b.slot(RING), :, :], max_rows[:, :]).then_inc(max_in[b.slot()], DMA)

            def cross_step(s):
                if s.c > -2:
                    load_inputs(s + 3)
                load_max(s)
                load_stack(s + 2)
                if s.k is None and s.c == -2:
                    fill(1)
                if s.k is None and s.c == -1:
                    sp.dma_start(wqkv_rows[:, :, :], W_qkv.rearrange("(n p) c -> p n c", p=P)).then_inc(S["qkv_in"], DMA)
                    sp.dma_start(wgate_rows[:, :], W_gate).then_inc(S["qkv_in"], DMA)
                    load_x(4, B, S["x_rest"])
                if s.k is None and s.c == 0:
                    fill(2)
                    fill(3)
                write_levels(s + 3)
                if joins(s, 0, 0):
                    causal_step(Batch(s.c - JOIN))

            def write_f_levels(b):
                if not live(b):
                    return
                wait_apart(sp, loaded, (S["f_q_low"], b.times(1, 1)))
                for t in range(PT):
                    n = DF // PT
                    sp.dma_start(qf_levels[b.index][:, t * n:(t + 1) * n].rearrange("l d h c -> (d h) l c"),
                                 qf_lev[:, :, t * T:(t + 1) * T]).then_inc(f_levels_out[b.slot()], DMA)

            def load_f_stack(b):
                if not live(b):
                    return
                wait_apart(sp, loaded, (f_levels_out[b.slot()], b.uses(PT * DMA, PT * DMA)))
                for pair, level, n in Q_RUNS:
                    sp.dma_start(q_stack[pair * DF:(pair + n) * DF, b.slot(RING), :, 0:T],
                                 qf_levels[b.index][level:level + n].rearrange("l d h c -> (l d) h c"))\
                        .then_inc(f_stack_in[b.slot()], DMA)

            def load_f_max(b):
                if not live(b):
                    return
                wait_apart(sp, loaded, (S["f_maxT_copied"], b.times(1, 1)))
                sp.dma_start(q_stack[MAX_ROW:ROWS, b.slot(RING), :, 0:T], maxf_rows[:, :])\
                    .then_inc(f_max_in[b.slot()], DMA)

            def store(b):
                if not live(b):
                    return
                wait_apart(sp, loaded, (S["f_out_ready"], b.times(1, 1)))
                sp.dma_start(out[b.index], xs[:, b.index, :]).then_inc(out_written, DMA)

            def causal_step(s):
                load_f_stack(s + 2)
                load_f_max(s + 1)
                write_f_levels(s + 3)
                store(s + -1)

            schedule(sp, cross_step, causal_step)
            for i in range(2):
                sp.wait_ge(levels_out[i], B // 2 * DMA)
                sp.wait_ge(f_levels_out[i], B // 2 * PT * DMA)
            sp.wait_ge(S["aug_written"], 2 * LEVELS * DMA)
            sp.wait_ge(out_written, B * DMA)

        @block.gpsimd
        def _(pool):
            chain = Chain(pool, S["pool_chain"])
            nc.gpsimd.memset(one_rows[:, :], 1.0).then_inc(S["fill_ready"], 1)
            chain(nc.gpsimd.memset(ident[:, :], 0.0))
            chain(nc.gpsimd.affine_select(out=ident[:, :], in_=ident[:, :], compare_op=ALU.not_equal, fill=1.0, base=0,
                                          pattern=[[-1, P]], channel_multiplier=1))
            nc.gpsimd.tensor_copy(ident_bf[:, :], ident[:, :]).then_inc(S["const_ready"], 1)
            nc.gpsimd.memset(ones_row[:, :], 1.0).then_inc(S["const_ready"], 1)
            chain(nc.gpsimd.memset(half_power[:, :], -0.5))

            def inverse_std(r, ready, signal, b):
                pool.wait_ge(ready, b.times(1, 1))
                nc.gpsimd.tensor_tensor(r[:, 1:2], r[:, 0:1], half_power[:, :], ALU.pow).then_inc(signal, 1)

            def fill_values():
                chain(nc.gpsimd.memset(v_cols[:, RING // 2:RING], 0.0))
                pool.wait_ge(S["vcols_zero"], 1)
                for n in range(RING):
                    for slot in range(2):
                        view = v_cols[:, n, :, :, :].rearrange("p t (r s j) x -> p (t r) s j x", s=2, j=GROUPS)
                        last = nc.gpsimd.memset(view[:, :, slot, :, 2 * DX + slot:2 * DX + slot + 1], 1.0)
                        last.then_inc(S["vcols_ready"], 1)
                pool.wait_ge(S["vcols_ready"], 2 * RING)

            def fill_causal():
                chain(nc.gpsimd.memset(causal_bf[:, :], 0.0))
                chain(nc.gpsimd.affine_select(out=causal_bf[:, :], in_=causal_bf[:, :], compare_op=ALU.is_ge, fill=-1e30,
                                              base=0, pattern=[[-1, P]], channel_multiplier=1))
                chain(nc.gpsimd.memset(vf_cols[:, :, :], 0.0))
                chain(nc.gpsimd.memset(vf_cols[:, :, DF:DF + 1], 1.0))
                for h in range(H):
                    nc.gpsimd.memset(first_head[:, h:h + 1], float(H - h))
                nc.gpsimd.memset(kf_rows[:, :], 1.0).then_inc(S["causal_ready"], 1)

            def cross_step(s):
                new = s + 3
                for b in moments_due(s):
                    inverse_std(rstd[:, b.slot(), :], S["norm_stats"], S["rstd_ready"], b)
                if s.k is None and s.c == -3:
                    fill_values()
                if s.k is None and s.c == -1:
                    fill_causal()
                if live(new):
                    pool.wait_ge(S["qk_copied"], new.times(2, 2))
                    pool.wait_ge(in_loaded[new.slot()], new.uses(2 * DMA, 2 * DMA))
                    nc.gpsimd.tensor_tensor(qk_f[:, :, :], qk_raw[:, :, :],
                                            mask_all[:, new.slot(), :].unsqueeze(1).to_broadcast([P, 2, C]),
                                            ALU.mult).then_inc(S["qk_masked"], 1)
                    pool.wait_ge(S["qk_high"], new.times(2, 2))
                    nc.gpsimd.tensor_tensor(qk_rest[:, :, :], qk_f[:, :, :], qk_levels[:, :, 0, :], ALU.subtract)\
                        .then_inc(S["qk_resid"], 1)
                    pool.wait_ge(S["v_added"], new.times(1, 1))
                    if new.k is None and new.c == 0:
                        pool.wait_ge(S["maskcol_ready"], 1)
                    reached(pool, S["pv_done"], new, 4, -12)
                    for t in range(PT):
                        for slot in range(2):
                            dst = v_cols[:, new.slot(RING), t, :, :].rearrange("p (r s j) x -> p r s j x", s=2, j=GROUPS)
                            src = v_sum[:, t, :].rearrange("p (r s j d) -> p r s j d", s=2, j=GROUPS, d=DX)
                            col = mask_col[:, bass.ds(new.times(PT, t), 1)]
                            last = nc.gpsimd.tensor_tensor(
                                dst[:, :, slot, :, slot * DX:(slot + 1) * DX], src[:, :, slot, :, :],
                                col.unsqueeze(2).unsqueeze(3).to_broadcast([P, 2, GROUPS, DX]), ALU.mult)
                    last.then_inc(S["v_ready"], 1)
                    pool.wait_ge(S["qk_mid"], new.times(2, 2))
                    nc.gpsimd.tensor_tensor(qk_levels[:, :, 2, :], qk_rest[:, :, :], qk_levels[:, :, 1, :], ALU.subtract)\
                        .then_inc(S["qk_low"], 1)
                if joins(s, 0, 0):
                    causal_step(Batch(s.c - JOIN))

            def causal_step(s):
                before, new = s + -1, s + 3

                def mask_probs(b, n):
                    wait_apart(pool, (S["fill_ready"], 2), (S["f_exp_done"], b.times(4, n + 1)))
                    part = probs_f[:, b.slot(), n * BANK:(n + 1) * BANK]
                    nc.gpsimd.affine_select(out=part, in_=part, compare_op=ALU.is_ge, fill=0.0, base=0,
                                            pattern=[[0, GROUPS], [1, T]], channel_multiplier=-1)\
                        .then_inc(S["f_masked"], 1)

                if live(new):
                    inverse_std(rstd_f, S["f_stats"], S["f_rstd"], new)
                if live(s):
                    for n in range(4):
                        mask_probs(s, n)
                if live(new):
                    pool.wait_ge(S["f_q_high"], new.times(1, 1))
                    nc.gpsimd.tensor_tensor(qf_rest[:, :], qf_f[:, :], qf_lev[:, 0, :], ALU.subtract)\
                        .then_inc(S["f_q_resid"], 1)
                    pool.wait_ge(S["f_q_mid"], new.times(1, 1))
                    nc.gpsimd.tensor_tensor(qf_lev[:, 2, :], qf_rest[:, :], qf_lev[:, 1, :], ALU.subtract)\
                        .then_inc(S["f_q_low"], 1)
                if live(before):
                    pool.wait_ge(S["f_y_ready"], before.times(1, 1))
                    nc.gpsimd.tensor_tensor(xs[:, before.index, :], y_f[:, :], xs[:, before.index, :], ALU.add)\
                        .then_inc(S["f_out_ready"], 1)

            schedule(pool, cross_step, causal_step)

        @block.tensor
        def _(pe):
            mm = nc.tensor.matmul

            pe.wait_ge(S["weights_in"], 3 * DMA)
            pe.wait_ge(S["const_ready"], 2)
            for n in range(3):
                last = nc.tensor.transpose(psum[:, BANK_A, n * P:(n + 1) * P], w_rows[:, n, :], ident[:, :])
            last.then_inc(S["w_transposed"], 1)
            pe.wait_ge(S["bias_ordered"], 2)
            for n in range(2):
                last = mm(psum[:, BANK_B, n:n + 1], bias_perm[0:1, n, :], ones_row[0:1, 0:1], start=True, stop=True)
            last.then_inc(S["bias_mm"], 1)
            pe.wait_ge(S["w_copied"], 3)

            def turn_mask():
                pe.wait_ge(S["maskrow_in"], DMA)
                nc.tensor.transpose(psum[:, bank_max[0], 0:B * PT], mask_rows[:, :], ident[0:B * PT, 0:B * PT])\
                    .then_inc(S["maskT_mm"], 1)

            def project_qk(b, turned):
                pe.wait_ge(S["xn_ready"], b.times(1, 1))
                pe.wait_ge(in_loaded[b.slot()], b.uses(2 * DMA, 2 * DMA))
                if turned:
                    pe.wait_ge(S["maxT_copied"], turned.times(1, 1))
                reached(pe, S["v_added"], b, 1)
                mm(psum[:, BANK_C, 0:C], wT[:, 0, :], xn[:, :], start=True, stop=True)
                mm(psum[:, BANK_C, C:2 * C], wT[:, 1, :], ctx[:, b.slot(), :], start=True, stop=True)\
                    .then_inc(S["qk_mm"], 1)

            def project_v(b):
                pe.wait_ge(S["qk_copied"], b.times(2, 2))
                for t in range(PT):
                    last = mm(psum[:, BANK_C, t * P:(t + 1) * P], ctx[:, b.slot(), t * P:(t + 1) * P], wT[:, 2, :],
                              start=True, stop=True)
                last.then_inc(S["v_mm"], 1)

            def max_scores(b, h):
                if h == 0:
                    if b.k is None and b.c in (0, 1):
                        pe.wait_ge(S[f"filled_{b.c}"], 3 * DMA)
                    pe.wait_ge(stack_in[b.slot()], b.uses(STACK_DMAS * DMA, STACK_DMAS * DMA))
                reached(pe, S["max_taken"], b, H, h + 1 - len(bank_max))
                for t in range(PT):
                    last = mm(psum[:, bank_max[h % len(bank_max)], t * C:(t + 1) * C],
                              q_stack[0:MAX_ROW, b.slot(RING), h, t * P:(t + 1) * P],
                              k_stack[0:MAX_ROW, b.slot(RING), h, :], start=True, stop=True)
                last.then_inc(S["scores_max"], 1)

            def turn_max(b):
                pe.wait_ge(S["max_split"], b.times(1, 1))
                nc.tensor.transpose(psum[0:LEVELS * H * PT, BANK_C, 0:P // 2].bitcast(BF16), max_levels[:, :],
                                    ident_bf[:, :]).then_inc(S["maxT_mm"], 1)

            def exp_scores(b, h):
                if h == 0:
                    pe.wait_ge(max_in[b.slot()], b.uses(DMA, DMA))
                reached(pe, S["exp_done"], b, H, h - 1)
                for t in range(PT):
                    last = mm(psum[:, bank_exp[h % 2], t * C:(t + 1) * C],
                              k_stack[0:ROWS, b.slot(RING), h, t * P:(t + 1) * P],
                              q_stack[0:ROWS, b.slot(RING), h, :], start=True, stop=True)
                last.then_inc(S["scores_exp"], 1)

            def value_product(b, quad, t):
                region = quad // 2
                if t == 0:
                    pe.wait_ge(S["exp_done"], b.times(H, GROUPS * (quad + 1)))
                    if quad == 0:
                        pe.wait_ge(S["v_ready"], b.times(1, 1))
                        reached(pe, S["pv_copied"], b, 1)
                for j in range(GROUPS):
                    last = mm(psum[j * 32:(j + 1) * 32, BANK_PV, region * C:(region + 1) * C],
                              v_cols[:, b.slot(RING), t, GROUPS * quad + j, :],
                              probs[:, quad % 2, j, t * C:(t + 1) * C],
                              start=(quad % 2 == 0 and t == 0), stop=(quad % 2 == 1 and t == PT - 1),
                              skip_group_check=True)
                if t == PT - 1:
                    last.then_inc(S["pv_done"], 1)

            def turn_outputs(b):
                if b.k is None and b.c == B - 1:
                    pe.wait_ge(S["x_updated"], b.c)
                pe.wait_ge(S["pv_copied"], b.times(1, 1))
                for t in range(PT):
                    for r in range(2):
                        n = t * 2 + r
                        last = nc.tensor.transpose(psum[:, BANK_C, n * P:(n + 1) * P],
                                                   pv_out[:, r * C + t * P:r * C + (t + 1) * P], ident[:, :])
                last.then_inc(S["outT_mm"], 1)

            def turn_back(b):
                pe.wait_ge(S["attn_normed"], b.times(1, 1))
                for t in range(PT):
                    last = nc.tensor.transpose(psum[:, BANK_C, t * P:(t + 1) * P], attn_t[:, t, :], ident[:, :])
                last.then_inc(S["attnT_mm"], 1)

            def turn_ffn_weights():
                pe.wait_ge(S["qkv_in"], 2 * DMA)
                for part, bank in enumerate((bank_exp[0], bank_exp[1], BANK_PV)):
                    for c in range(PT):
                        for t in range(PT):
                            last = nc.tensor.transpose(psum[:, bank, c * C + t * P:c * C + (t + 1) * P],
                                                       wqkv_rows[:, part * PT + t, c * P:(c + 1) * P], ident[:, :])
                for c in range(PT):
                    last = nc.tensor.transpose(psum[:, BANK_C, c * H:(c + 1) * H],
                                               wgate_rows[:, c * P:(c + 1) * P], ident[0:H, 0:H])
                last.then_inc(S["wf_transposed"], 1)

            def cross_step(s):
                before, nxt, new = s + -1, s + 1, s + 3
                if s.k is None and s.c == -1:
                    pe.wait_ge(S["maskcol_ready"], 1)
                joined = s.k is None and s.c > JOIN - 3
                for h in range(H):
                    if live(nxt):
                        max_scores(nxt, h)
                    b, e = lagged(s, h, LAG, H)
                    quad, j = divmod(e, GROUPS)
                    if live(b):
                        exp_scores(b, e)
                    if j % 2:
                        b, q = (b + -1, GROUPS - 1) if quad == 0 else (b, quad - 1)
                        if live(b):
                            value_product(b, q, j // 2)
                    if h == 3 and live(s):
                        turn_max(s)
                    if h == 4 and s.k is None and s.c == 0:
                        pe.wait_ge(S["maxT_copied"], 1)
                        turn_ffn_weights()
                    if h == 6 and live(new):
                        if s.k is None and s.c == 0:
                            pe.wait_ge(S["wf_copied"], 5)
                        project_qk(new, s if live(s) else None)
                    if h == 7 and s.k is None and s.c == -3:
                        turn_mask()
                    if h == 9 and live(new):
                        project_v(new)
                    if h == 12 and live(before):
                        if live(new):
                            pe.wait_ge(S["v_added"], new.times(1, 1))
                        elif live(s):
                            pe.wait_ge(S["maxT_copied"], s.times(1, 1))
                        if joined:
                            pe.wait_ge(S["f_q_copied"], s.c - JOIN + 4)
                        turn_outputs(before)
                    if h == 15 and live(before):
                        turn_back(before)
                    if joins(s, h, JOIN_HEAD):
                        causal_step(Batch(s.c - JOIN))
                if s.k is None and s.c == 0:
                    pe.wait_ge(S["filled_rest"], 2 * 3 * DMA)

            def f_turn_x(b):
                pe.wait_ge(S["f_xn"], b.times(1, 1))
                for c in range(PT):
                    last = nc.tensor.transpose(psum[:, BANK_B, c * T:(c + 1) * T], xn_f[:, c * P:(c + 1) * P], ident[:, :])
                last.then_inc(S["f_xnT_mm"], 1)

            def f_project_kv(b):
                reached(pe, S["f_selected"], b, 1)
                for c in range(PT):
                    last = mm(psum[:, BANK_A, :], xnT[:, c, :], wfT[:, c, C:3 * C], start=(c == 0), stop=(c == PT - 1))
                last.then_inc(S["f_kv_mm"], 1)

            def f_project_gq(b):
                pe.wait_ge(S["f_xnT"], b.times(1, 1))
                if b.k is None and b.c < 4:
                    pe.wait_ge(S["x_updated"], (B - 2, B - 2, B - 1, B)[b.c])
                    pe.wait_ge(S["maxT_copied"], B - 1 if b.c == 0 else B)
                for c in range(PT):
                    mm(psum[:, BANK_C, PT * T:PT * T + H], xnT[:, c, :], wgT[:, c, :], start=(c == 0), stop=(c == PT - 1))
                for t in range(PT):
                    for c in range(PT):
                        last = mm(psum[:, BANK_C, t * T:(t + 1) * T], wfT[:, c, t * P:(t + 1) * P], xnT[:, c, :],
                                  start=(c == 0), stop=(c == PT - 1))
                last.then_inc(S["f_gq_mm"], 1)

            def f_turn_k(b):
                pe.wait_ge(S["f_kT_in"], b.times(1, 1))
                nc.tensor.transpose(psum[0:ROWS, bank_max[0], 0:T // 2].bitcast(BF16), kf_rows[:, :],
                                    ident_bf[:, :]).then_inc(S["f_kT_mm"], 1)

            def f_max_scores(b, n):
                if n == 0:
                    pe.wait_ge(S["f_kT"], b.times(1, 1))
                    pe.wait_ge(f_stack_in[b.slot()], b.uses(len(Q_RUNS) * DMA, len(Q_RUNS) * DMA))
                if n == 1:
                    reached(pe, S["f_maxT_copied"], b, 1)
                reached(pe, S["f_max_taken"], b, 4, n - 1)
                bank = bank_max[n % CAUSAL_MAX_BANKS]
                mm(psum[:, bank, :].rearrange("p (h t) -> p h t", h=GROUPS), ident_bf[:, :],
                   causal_bf[:, :].unsqueeze(1).to_broadcast([P, GROUPS, T]), start=True, stop=False,
                   skip_group_check=True)
                for j in range(GROUPS):
                    last = mm(psum[:, bank, j * T:(j + 1) * T],
                              q_stack[0:MAX_ROW, b.slot(RING), GROUPS * n + j, 0:T],
                              kf_stack[0:MAX_ROW, b.slot(RING), :], start=False, stop=(j == GROUPS - 1),
                              skip_group_check=True)
                last.then_inc(S["f_scores_max"], 1)

            def f_turn_max(b):
                wait_apart(pe, (S["causal_ready"], 1), (S["f_max_split"], b.times(1, 1)))
                nc.tensor.transpose(psum[0:LEVELS * H, bank_max[1], 0:P // 2].bitcast(BF16), maxf_levels[:, :],
                                    ident_bf[:, :]).then_inc(S["f_maxT_mm"], 1)

            def f_exp_scores(b, n):
                if n == 0:
                    pe.wait_ge(f_max_in[b.slot()], b.uses(DMA, DMA))
                reached(pe, S["f_exp_done"], b, 4, n - 1)
                mm(psum[:, bank_exp[n % 2], :], kf_stack[:, b.slot(RING), :],
                   q_stack[:, b.slot(RING), GROUPS * n:GROUPS * (n + 1), 0:T], start=True, stop=True)\
                    .then_inc(S["f_scores_exp"], 1)

            def f_value_product(b):
                pe.wait_ge(S["f_masked"], b.times(4, 4))
                for n in range(GROUPS):
                    last = mm(psum[32 * n:32 * (n + 1), BANK_PV, :], vf_cols[:, b.slot(RING), :],
                              probs_f[:, b.slot(), n * BANK:(n + 1) * BANK], start=True, stop=True)
                last.then_inc(S["f_pv_done"], 1)

            def f_turn_outputs(b):
                pe.wait_ge(S["f_pv_copied"], b.times(1, 1))
                for j in range(GROUPS):
                    last = nc.tensor.transpose(psum[:, BANK_B, j * P:(j + 1) * P], pvf_out[:, j * T:(j + 1) * T],
                                               ident[:, :])
                last.then_inc(S["f_outT_mm"], 1)

            def causal_step(s):
                before, nxt, nxt2, new = s + -1, s + 1, s + 2, s + 3
                if s.k is None and s.c == -3:
                    pe.wait_ge(S["causal_ready"], 1)
                    pe.wait_ge(S["max_taken"], H * B)
                for n in range(4):
                    if live(s):
                        f_exp_scores(s, n)
                    if live(nxt):
                        f_max_scores(nxt, n)
                    if n == 2 and live(new):
                        f_turn_x(new)
                if live(new):
                    f_project_gq(new)
                if live(before):
                    if not live(new):
                        reached(pe, S["f_y_ready"], before, 1)
                    f_turn_outputs(before)
                if live(nxt):
                    f_turn_max(nxt)
                if live(s):
                    f_value_product(s)
                if live(new):
                    f_project_kv(new)
                if live(nxt2):
                    f_turn_k(nxt2)

            schedule(pe, cross_step, causal_step)

        @block.scalar
        def _(act):
            def copy(dst, src, bias=0.0, scale=1.0, function=ACT.Copy):
                return nc.scalar.activation(dst, src, function, bias=bias, scale=scale)

            act.wait_ge(S["bias_in"], 2 * DMA)
            for n, scale in enumerate((XATTN_SCALE, 1.0)):
                copy(bias_perm[:, n, :].rearrange("a (d h) -> a d h", h=H),
                     bias_rows[:, n, :].rearrange("a (h d) -> a d h", d=DX), scale=scale).then_inc(S["bias_ordered"], 1)
            act.wait_ge(S["bias_mm"], 1)
            for n in range(2):
                copy(bias_col[:, n:n + 1], psum[:, BANK_B, n:n + 1]).then_inc(S["bias_copied"], 1)

            def cross_step(s):
                before, nxt, new = s + -1, s + 1, s + 3

                def copy_max(b):
                    act.wait_ge(S["maxT_mm"], b.times(1, 1))
                    if b.c >= 1:
                        last = b + -1
                        act.wait_ge(max_in[last.slot()], last.uses(DMA, DMA))
                    copy(max_rows[:, :], psum[0:LEVELS * H * PT, BANK_C, 0:P // 2].bitcast(BF16))\
                        .then_inc(S["maxT_copied"], 1)

                for h in range(H):
                    b, e = lagged(s, h, LAG, H)
                    quad, j = divmod(e, GROUPS)
                    if live(b):
                        act.wait_ge(S["scores_exp"], b.times(H, e + 1))
                        if j == 0:
                            reached(act, S["pv_done"], b, 4, quad - 1)
                        nc.scalar.activation(probs[:, quad % 2, j, :], psum[:, bank_exp[e % 2], :], ACT.Exp)\
                            .then_inc(S["exp_done"], 1)
                    if h == 3 and live(s):
                        copy_max(s)
                    if h == 10 and live(before):
                        act.wait_ge(S["pv_done"], before.times(4, 4))
                        copy(pv_out[:, :], psum[:, BANK_PV, :]).then_inc(S["pv_copied"], 1)
                    if h == 4 and s.k is None and s.c == 0:
                        act.wait_ge(S["wf_transposed"], 1)
                        for c in range(PT):
                            copy(wfT[:, c, 0:C].rearrange("p (d h) -> p h d", h=H),
                                 psum[:, bank_exp[0], c * C:(c + 1) * C].rearrange("p (h d) -> p h d", h=H),
                                 scale=FFN_SCALE).then_inc(S["wf_copied"], 1)
                        for n, bank in enumerate((bank_exp[1], BANK_PV)):
                            copy(wfT[:, :, (n + 1) * C:(n + 2) * C],
                                 psum[:, bank, :].rearrange("p (c o) -> p c o", c=PT)).then_inc(S["wf_copied"], 1)
                        copy(wgT[:, :, :], psum[:, BANK_C, 0:PT * H].rearrange("p (c h) -> p c h", c=PT))\
                            .then_inc(S["wf_copied"], 1)
                    if h in (6, 7) and live(new):
                        if h == 6:
                            act.wait_ge(S["qk_mm"], new.times(1, 1))
                            if s.k is None and s.c == -3:
                                act.wait_ge(S["bias_copied"], 2)
                        n = h - 6
                        copy(qk_raw[:, n, :], psum[:, BANK_C, n * C:(n + 1) * C], bias=bias_col[:, n:n + 1],
                             function=ACT.Identity).then_inc(S["qk_copied"], 1)
                    if h == 7 and s.k is None and s.c == -3:
                        act.wait_ge(S["maskT_mm"], 1)
                        copy(mask_col[:, :], psum[:, bank_max[0], 0:B * PT]).then_inc(S["maskcol_ready"], 1)
                        act.wait_ge(S["gates_in"], 2 * DMA)
                        nc.scalar.activation(gates[:, :], gates_in[:, :], ACT.Tanh).then_inc(S["tanh_done"], 1)
                    if h in (10, 11) and live(new):
                        if h == 10:
                            if new.c >= 1:
                                last = new + -1
                                act.wait_ge(levels_out[last.slot()], last.uses(DMA, DMA))
                            act.wait_ge(S["qk_masked"], new.times(1, 1))
                        n = h - 10
                        copy(qk_levels[:, n, 0, :], qk_f[:, n, :]).then_inc(S["qk_high"], 1)
                    if h in (13, 14) and live(new):
                        if h == 13:
                            act.wait_ge(S["qk_resid"], new.times(1, 1))
                        n = h - 13
                        copy(qk_levels[:, n, 1, :], qk_rest[:, n, :]).then_inc(S["qk_mid"], 1)
                    if joins(s, h, JOIN_HEAD):
                        causal_step(Batch(s.c - JOIN))

            def causal_step(s):
                before, nxt, nxt2, new = s + -1, s + 1, s + 2, s + 3

                if live(nxt2):
                    act.wait_ge(S["f_logit"], nxt2.times(1, 1))
                    nc.scalar.activation(gate_e[:, :], logit[:, :], ACT.Exp, bias=top_neg[:, 0:1],
                                         accum_out=gate_sum[:, 0:1]).then_inc(S["f_gate_e"], 1)
                for n in range(4):
                    if n == 2 and live(new):
                        act.wait_ge(S["f_xnT_mm"], new.times(1, 1))
                        copy(xnT[:, :, :], psum[:, BANK_B, 0:PT * T].rearrange("p (c t) -> p c t", c=PT))\
                            .then_inc(S["f_xnT"], 1)
                    if live(s):
                        act.wait_ge(S["f_scores_exp"], s.times(4, n + 1))
                        nc.scalar.activation(probs_f[:, s.slot(), n * BANK:(n + 1) * BANK], psum[:, bank_exp[n % 2], :],
                                             ACT.Exp).then_inc(S["f_exp_done"], 1)
                if live(new):
                    act.wait_ge(S["f_gq_mm"], new.times(1, 1))
                    reached(act, S["f_q_low"], new, 1)
                    copy(logit[:, :], psum[:, BANK_C, PT * T:PT * T + H])
                    copy(qf_f[:, :], psum[:, BANK_C, 0:PT * T]).then_inc(S["f_q_copied"], 1)
                    act.wait_ge(S["f_q_copied"], new.times(1, 1))
                    if new.c >= 1:
                        last = new + -1
                        act.wait_ge(f_levels_out[last.slot()], last.uses(PT * DMA, PT * DMA))
                    copy(qf_lev[:, 0, :], qf_f[:, :]).then_inc(S["f_q_high"], 1)
                if live(nxt):
                    act.wait_ge(S["f_maxT_mm"], nxt.times(1, 1))
                    if nxt.c >= 1:
                        last = nxt + -1
                        act.wait_ge(f_max_in[last.slot()], last.uses(DMA, DMA))
                    copy(maxf_rows[:, :], psum[0:LEVELS * H, bank_max[1], 0:P // 2].bitcast(BF16))\
                        .then_inc(S["f_maxT_copied"], 1)
                if live(s):
                    act.wait_ge(S["f_pv_done"], s.times(1, 1))
                    copy(pvf_out[:, :], psum[:, BANK_PV, :]).then_inc(S["f_pv_copied"], 1)
                if live(new):
                    act.wait_ge(S["f_q_resid"], new.times(1, 1))
                    copy(qf_lev[:, 1, :], qf_rest[:, :]).then_inc(S["f_q_mid"], 1)
                if live(nxt2):
                    act.wait_ge(S["f_kT_mm"], nxt2.times(1, 1))
                    copy(kf_stack[:, nxt2.slot(RING), :], psum[0:ROWS, bank_max[0], 0:T // 2].bitcast(BF16))\
                        .then_inc(S["f_kT"], 1)

            schedule(act, cross_step, causal_step)

        @block.vector
        def _(dve):
            chain = Chain(dve, S["dve_chain"])
            v = nc.vector

            v.memset(zero_rows[:, :], 0.0).then_inc(S["fill_ready"], 1)
            v.memset(v_cols[:, 0:RING // 2], 0.0).then_inc(S["vcols_zero"], 1)

            def copy_weights():
                dve.wait_ge(S["w_transposed"], 1)
                v.tensor_scalar(wT[:, 0, :].rearrange("p (d h) -> p h d", h=H),
                                psum[:, BANK_A, 0:P].rearrange("p (h d) -> p h d", h=H),
                                XATTN_SCALE, None, ALU.mult).then_inc(S["w_copied"], 1)
                v.tensor_copy(wT[:, 1, :].rearrange("p (d h) -> p h d", h=H),
                              psum[:, BANK_A, P:2 * P].rearrange("p (h d) -> p h d", h=H)).then_inc(S["w_copied"], 1)
                v.tensor_copy(wT[:, 2, :], psum[:, BANK_A, 2 * P:3 * P]).then_inc(S["w_copied"], 1)

            def split_mask():
                dve.wait_ge(S["mask_in"], DMA)
                v.tensor_copy(aug_f[:, 0, :], mask_b[:, :])
                chain(v.tensor_scalar(aug_f[:, 1, :], mask_b[:, :], 1.0, NEG, ALU.subtract, ALU.mult))
                chain(v.tensor_copy(aug_levels[:, :, 0, :], aug_f[:, :, :]))
                chain(v.tensor_tensor(aug_r[:, :, :], aug_f[:, :, :], aug_levels[:, :, 0, :], ALU.subtract))
                chain(v.tensor_copy(aug_levels[:, :, 1, :], aug_r[:, :, :]))
                v.tensor_tensor(aug_levels[:, :, 2, :], aug_r[:, :, :], aug_levels[:, :, 1, :], ALU.subtract)\
                    .then_inc(S["aug_ready"], 1)

            def split_max(part, neg, levels, rest, signal, mark):
                n = neg.shape[1]
                if mark is not None:
                    chain.passed(mark)
                if part == 0:
                    return chain.mark(v.tensor_copy(levels[:, 0:n], neg))
                if part == 1:
                    return chain.mark(v.tensor_tensor(rest, neg, levels[:, 0:n], ALU.subtract))
                if part == 2:
                    return chain.mark(v.tensor_copy(levels[:, n:2 * n], rest))
                v.tensor_tensor(levels[:, 2 * n:3 * n], rest, levels[:, n:2 * n], ALU.subtract).then_inc(signal, 1)

            def moments(part, b, st, mv, r, signal, mark=None):
                if part == 0:
                    return chain.mark(v.bn_stats(st, xs[:, b.index, :]))
                if part == 1:
                    wait_apart(dve, (S["fill_ready"], 1), (S["dve_chain"], chain.base + mark))
                    return chain.mark(v.bn_aggr(mv, st))
                chain.passed(mark)
                v.tensor_scalar(r[:, 0:1], mv[:, 1:2], EPS, None, ALU.add).then_inc(signal, 1)

            def normalise(b, dst, mv, r, signal):
                v.tensor_scalar(dst[:, :], xs[:, b.index, :], mv[:, 0:1], r[:, 1:2], ALU.subtract, ALU.mult)\
                    .then_inc(signal, 1)

            def normalise_outputs(part, b, mark=None):
                rows = psum[:, BANK_C, :].rearrange("p (g j x) -> p g j x", g=2 * PT, j=GROUPS)
                if part == 0:
                    dve.wait_ge(S["outT_mm"], b.times(1, 1))
                    return chain.mark(v.reciprocal(recip[:, :].rearrange("p (g j s) -> p g j s", g=2 * PT, j=GROUPS),
                                                   rows[:, :, :, 2 * DX:2 * DX + 2]))
                chain.passed(mark)
                if part == 1:
                    return chain.mark(v.tensor_tensor(
                        recip_g[:, :].rearrange("p (t n) -> p t n", t=PT), recip[:, :].rearrange("p (t n) -> p t n", t=PT),
                        mask_gate[:, bass.ds(b.times(PT), PT)].unsqueeze(2).to_broadcast([P, PT, 2 * 8]), ALU.mult))
                dst = attn_t[:, :, :].rearrange("p t (r s j d) -> p (t r) s j d", r=2, s=2, j=GROUPS)
                scale = recip_g[:, :].rearrange("p (g j s) -> p g j s", g=2 * PT, j=GROUPS)
                for slot in range(2):
                    last = v.tensor_tensor(dst[:, :, slot, :, :], rows[:, :, :, slot * DX:(slot + 1) * DX],
                                           scale[:, :, :, slot].unsqueeze(3).to_broadcast([P, 2 * PT, GROUPS, DX]),
                                           ALU.mult)
                last.then_inc(S["attn_normed"], 1)

            def cross_step(s):
                before, nxt, new = s + -1, s + 1, s + 3
                split = stat = norm = None

                def split_part(part, mark):
                    return split_max(part, neg_max[:, s.slot(), :], max_levels, max_rest[:, :], S["max_split"], mark)

                def moments_part(part, mark=None, b=new):
                    i = b.slot()
                    return moments(part, b, stats[:, i, :], meanvar[:, i, :], rstd[:, i, :], S["norm_stats"], mark)

                if live(s):
                    dve.wait_ge(S["max_taken"], s.times(H, H))
                    split = split_part(0, None)
                for b in moments_due(s):
                    if s.k is None and b.c == 2:
                        dve.wait_ge(S["x_second"], DMA)
                    if s.k is None and b.c == 0:
                        dve.wait_ge(S["x_first"], DMA)
                    stat = moments_part(0, None, b)
                    if s.k is None:
                        moments_part(2, moments_part(1, stat, b), b)
                if s.k is None and s.c == -3:
                    copy_weights()
                if live(s):
                    split = split_part(1, split)
                for h in range(H):
                    if live(nxt):
                        dve.wait_ge(S["scores_max"], nxt.times(H, h + 1))
                        v.tensor_reduce(out=neg_max[:, nxt.slot(), h * PT:(h + 1) * PT],
                                        in_=psum[:, bank_max[h % len(bank_max)], :]
                                        .rearrange("p (t c) -> p t c", t=PT), op=ALU.max, axis=AX.X, negate=True)\
                            .then_inc(S["max_taken"], 1)
                    if joins(s, h, 3):
                        causal_step(Batch(s.c - JOIN))
                    if h == 0:
                        if live(s):
                            split = split_part(2, split)
                        if s.k is not None:
                            stat = moments_part(1, stat)
                        if live(s):
                            split_part(3, split)
                    if h == 1:
                        if s.k is not None:
                            moments_part(2, stat)
                    if h == 3 and live(new):
                        dve.wait_ge(S["rstd_ready"], new.times(1, 1))
                        normalise(new, xn, meanvar[:, new.slot(), :], rstd[:, new.slot(), :], S["xn_ready"])
                    if h == 4 and s.k is None and s.c == -3:
                        split_mask()
                        dve.wait_ge(S["bv_in"], DMA)
                    if h == 4 and s.k is None and s.c == -1:
                        dve.wait_ge(S["maskcol_ready"], 1)
                        dve.wait_ge(S["tanh_done"], 1)
                        v.tensor_scalar(mask_gate[:, :], mask_col[:, :], gates[:, 0:1], None, ALU.mult)
                    if h == 8 and live(new):
                        dve.wait_ge(S["v_mm"], new.times(1, 1))
                        reached(dve, S["v_ready"], new, 1)
                        v.tensor_tensor(v_sum[:, :, :], psum[:, BANK_C, 0:PT * P].rearrange("p (t o) -> p t o", t=PT),
                                        bv_all[:, :].unsqueeze(1).to_broadcast([P, PT, P]), ALU.add)\
                            .then_inc(S["v_added"], 1)
                    if h == 12 and live(before):
                        norm = normalise_outputs(0, before)
                        norm = normalise_outputs(1, before, norm)
                    if h == 13 and live(before):
                        normalise_outputs(2, before, norm)
                    if h == 15 and live(before):
                        dve.wait_ge(S["attnT_mm"], before.times(1, 1))
                        v.tensor_tensor(xs[:, before.index, :], psum[:, BANK_C, 0:C], xs[:, before.index, :], ALU.add)\
                            .then_inc(S["x_updated"], 1)
                if s.k is None and s.c == 0:
                    dve.wait_ge(S["x_rest"], DMA)

            def choose_head(part, mark=None):
                if mark is not None:
                    chain.passed(mark)
                if part == 0:
                    return chain.mark(v.tensor_scalar(rank[:, :], logit[:, :], top_neg[:, 0:1], 0.0, ALU.add, ALU.is_ge))
                if part == 1:
                    return chain.mark(v.tensor_tensor(rank[:, :], rank[:, :], first_head[:, :], ALU.mult))
                if part == 2:
                    return chain.mark(v.tensor_reduce(out=rank_top[:, :], in_=rank[:, :], op=ALU.max, axis=AX.X))
                return chain.mark(v.tensor_scalar(chosen[:, :], rank[:, :], rank_top[:, 0:1], None, ALU.is_ge))

            def lay_out_k(part, mark):
                k_rows = kf_rows[:, 0:MAX_ROW].rearrange("p (g d) -> p g d", d=DF)
                kk = kv_one[:, 0, :].unsqueeze(1)
                chain.passed(mark)
                if part == 0:
                    return chain.mark(v.tensor_copy(k_rows[:, 0:3, :], kk.to_broadcast([P, 3, DF])))
                if part == 1:
                    return chain.mark(v.tensor_tensor(kf_rest[:, :, :], kk.to_broadcast([P, 2, DF]), k_rows[:, 0:2, :],
                                                      ALU.subtract))
                if part == 2:
                    return chain.mark(v.tensor_copy(k_rows[:, 3:5, :], kf_rest[:, :, :]))
                v.tensor_tensor(k_rows[:, 5, :], kf_rest[:, 0, :], k_rows[:, 3, :], ALU.subtract).then_inc(S["f_kT_in"], 1)

            def finish(part, b, mark=None):
                rows = psum[:, BANK_B, :].rearrange("p (j g x) -> p j g x", j=GROUPS, g=GROUPS)
                if part == 0:
                    dve.wait_ge(S["f_outT_mm"], b.times(1, 1))
                    return chain.mark(v.reciprocal(recip_f[:, :].rearrange("p (j g) -> p j g", j=GROUPS), rows[:, :, :, DF]))
                if part == 1:
                    chain.passed(mark)
                    return chain.mark(v.tensor_scalar(recip_fg[:, :], recip_f[:, :], gates[:, 1:2], None, ALU.mult))
                if part == 2:
                    if b.k is None and b.c + 4 >= B:
                        reached(dve, S["f_out_ready"], b, 1)
                    chain.passed(mark)
                    v.tensor_tensor(y_f[:, :].rearrange("p (g j d) -> p j g d", g=GROUPS, j=GROUPS), rows[:, :, :, 0:DF],
                                    recip_fg[:, :].rearrange("p (j g) -> p j g", j=GROUPS).unsqueeze(3)
                                    .to_broadcast([P, GROUPS, GROUPS, DF]), ALU.mult).then_inc(S["f_y_ready"], 1)

            def causal_step(s):
                before, nxt, nxt2, new = s + -1, s + 1, s + 2, s + 3
                stat = split = kv = gate = head = norm = None

                def reduce_max(n):
                    if live(nxt):
                        dve.wait_ge(S["f_scores_max"], nxt.times(4, n + 1))
                        v.tensor_reduce(out=neg_max_f[:, n * GROUPS:(n + 1) * GROUPS],
                                        in_=psum[:, bank_max[n % CAUSAL_MAX_BANKS], :]
                                        .rearrange("p (h t) -> p h t", h=GROUPS), op=ALU.max, axis=AX.X, negate=True)\
                            .then_inc(S["f_max_taken"], 1)

                def split_part(part, mark=None):
                    if live(nxt):
                        return split_max(part, neg_max_f[:, :], maxf_levels, maxf_rest[:, :], S["f_max_split"], mark)

                def moments_part(part, mark=None):
                    if live(new):
                        return moments(part, new, stats_f[:, :], meanvar_f[:, :], rstd_f[:, :], S["f_stats"], mark)

                def choose_part(part, mark=None):
                    if live(nxt2):
                        return choose_head(part, mark)

                def lay_out_part(part, mark):
                    if live(nxt2):
                        return lay_out_k(part, mark)

                def finish_part(part, mark=None):
                    if live(before):
                        return finish(part, before, mark)

                if s.k is None and s.c == -3:
                    dve.wait_ge(S["causal_ready"], 1)
                stat = moments_part(0)
                if live(nxt2):
                    dve.wait_ge(S["f_q_copied"], nxt2.times(1, 1))
                    v.tensor_reduce(out=top_neg[:, 0:1], in_=logit[:, :], op=ALU.max, axis=AX.X, negate=True)\
                        .then_inc(S["f_logit"], 1)
                stat = moments_part(1, stat)
                if live(nxt2):
                    dve.wait_ge(S["f_logit"], nxt2.times(1, 1))
                head = choose_part(0)
                moments_part(2, stat)
                head = choose_part(1, head)
                reduce_max(0)
                head = choose_part(2, head)
                if live(new):
                    dve.wait_ge(S["f_rstd"], new.times(1, 1))
                    normalise(new, xn_f, meanvar_f, rstd_f, S["f_xn"])
                reduce_max(1)
                head = choose_part(3, head)
                reduce_max(2)
                reduce_max(3)
                if live(nxt):
                    dve.wait_ge(S["f_max_taken"], nxt.times(4, 4))
                split = split_part(0)
                if live(nxt2):
                    dve.wait_ge(S["f_gate_e"], nxt2.times(1, 1))
                    gate = chain.mark(v.reciprocal(gate_sum[:, 1:2], gate_sum[:, 0:1]))
                split = split_part(1, split)
                split = split_part(2, split)
                split_part(3, split)
                if live(nxt2):
                    chain.passed(head)
                    dve.wait_ge(S["f_kv_mm"], nxt2.times(1, 1))
                    v.tensor_tensor(kv_sel[:, :, :, :], psum[:, BANK_A, :].rearrange("p (k h d) -> p k h d", k=2, h=H),
                                    chosen[:, :].unsqueeze(1).unsqueeze(3).to_broadcast([P, 2, H, DF]), ALU.mult)\
                        .then_inc(S["f_selected"], 1)
                norm = finish_part(0)
                if live(nxt2):
                    dve.wait_ge(S["f_selected"], nxt2.times(1, 1))
                    kv = chain.mark(v.tensor_reduce(out=kv_one[:, :, :],
                                                    in_=kv_sel[:, :, :, :].rearrange("p k h d -> p k d h"),
                                                    op=ALU.add, axis=AX.X))
                norm = finish_part(1, norm)
                kv = lay_out_part(0, kv)
                if live(nxt2):
                    chain.passed(gate)
                    v.tensor_scalar(vf_cols[:, nxt2.slot(RING), 0:DF], kv_one[:, 1, :], gate_sum[:, 1:2], None, ALU.mult)
                kv = lay_out_part(1, kv)
                finish_part(2, norm)
                kv = lay_out_part(2, kv)
                lay_out_part(3, kv)

            schedule(dve, cross_step, causal_step, chain, 7, 16)


_INS = ['x', 'ctx_2048', 'mask_Bx1x2048_fk1', 'g_xattn', 'g_ffn', 'L0_xattn_Wq', 'L0_xattn_bq', 'L0_xattn_Wk',
        'L0_xattn_bk', 'L0_xattn_Wv', 'L0_xattn_bv', 'L0_ffn_W_gate', 'L0_ffn_W_qkv']


def kernel(**inputs):
    import numpy as _np
    import concourse.bacc as _bacc
    from concourse import mybir as _mybir
    from concourse.bass_utils import run_bass_kernel_spmd as _run

    nc = _bacc.Bacc("TRN2", target_bir_lowering=False, num_devices=1)
    arrays, args = {}, []
    for name in _INS:
        a = _np.ascontiguousarray(inputs[name])
        arrays[f"in_{name}"] = a
        args.append(nc.dram_tensor(f"in_{name}", a.shape, _mybir.dt.from_np(a.dtype), kind="ExternalInput").ap())
    x = inputs["x"]
    out = nc.dram_tensor("out", x.shape, _mybir.dt.float32, kind="ExternalOutput").ap()
    flamingo_kernel(nc, *args, out)
    r = _run(nc, [arrays], core_ids=[0])
    return r.results[0]["out"]
```
